# Optimizing a Trainium2 kernel written in Bass

```python
import numpy as np
import jax
import jax.numpy as jnp

def _softmax(x, axis=-1):
    return jax.nn.softmax(x, axis=axis)

def _gelu(x):
    return jax.nn.gelu(x, approximate=True)

def _silu(x):
    return jax.nn.silu(x)

def _sigmoid(x):
    return jax.nn.sigmoid(x)

def _layernorm(x, axis=-1, eps=1e-05):
    m = jnp.mean(x, axis=axis, keepdims=True)
    v = jnp.var(x, axis=axis, keepdims=True)
    return (x - m) / jnp.sqrt(v + eps)

def _scatter_add(tgt, idx, src, axis=0):
    return tgt.at[idx].add(src)

def _segment_sum(src, seg, n):
    return jax.ops.segment_sum(src, seg, n)
kernel_name = 'mk_xattn_ffn_d4_seqx_r4_07dc72'

def setup_inputs(seed: int=0):
    np.random.seed(seed)
    _w = jnp.asarray

    def _rec_inputs():
        import jax
        import jax.numpy as jnp
        _rk = jax.random.key(seed)
        x = -0.0003929 + 0.9999 * jax.random.normal(jax.random.fold_in(_rk, 1), (8, 256, 256), jnp.float32)
        _lenS = 256 - jax.random.randint(jax.random.fold_in(_rk, 7), (8,), 0, max(1, 256 // 4) + 1, jnp.int32)
        _lenS2 = 256 - jax.random.randint(jax.random.fold_in(_rk, 8), (8,), 0, max(1, 256 // 4) + 1, jnp.int32)
        _ctx_1024P = jax.random.normal(jax.random.fold_in(_rk, 11), (8, 16, 256), jnp.float32)
        _ctx_1024c = jax.random.dirichlet(jax.random.fold_in(_rk, 511), 0.3 * jnp.ones((16,), jnp.float32), (8, 256))
        _ctx_1024t = jnp.einsum('bsk,bkd->bsd', _ctx_1024c, _ctx_1024P)
        _ctx_1024t = _ctx_1024t * jax.lax.rsqrt(jnp.mean(jnp.square(_ctx_1024t)) + 1e-12) * 0.953939
        ctx_1024 = 2.81802e-05 + 1.00001 * (_ctx_1024t + 0.3 * jax.random.normal(jax.random.fold_in(_rk, 611), (8, 256, 256), jnp.float32))
        itok_SxS2_0_2016 = jax.random.randint(jax.random.fold_in(_rk, 12), (256, 256), 0, 2017, jnp.int32)
        return (x, ctx_1024, itok_SxS2_0_2016)
    x, ctx_1024, itok_SxS2_0_2016 = _rec_inputs()

    def _L0_xattn_setup():
        import jax, jax.numpy as jnp
        import numpy as np
        B, S, DIM, NH = (64, 64, 256, 8)
        DH = DIM // NH
        EPS = 1e-06
        LN_EPS = 1e-05

        def _make_hops(n):
            hops = np.zeros((n, n), dtype=np.int64)
            cur = 1
            for i in range(n):
                for j in range(i + 1, n):
                    hops[i, j] = cur
                    hops[j, i] = cur
                    cur += 1
            return (hops, cur)

        def _mlstm_forward(q, k, v, igate_w, igate_b, fgate_w, fgate_b, rpe, ln_w, ln_b, hops):
            Bq, Sq, _ = q.shape
            pos_emb = rpe[hops]
            gate_in = jnp.concatenate([q, k, v], axis=-1)
            ig = gate_in @ igate_w.T + igate_b
            fg = gate_in @ fgate_w.T + fgate_b
            ig = jnp.transpose(ig, (0, 2, 1))
            fg = jnp.transpose(fg, (0, 2, 1))
            qh = q.reshape(Bq, Sq, NH, DH).transpose(0, 2, 1, 3)
            kh = k.reshape(Bq, Sq, NH, DH).transpose(0, 2, 1, 3)
            vh = v.reshape(Bq, Sq, NH, DH).transpose(0, 2, 1, 3)
            log_f = jax.nn.log_sigmoid(fg)
            csum = jnp.cumsum(log_f, axis=-1)
            csum = jnp.concatenate([jnp.zeros((Bq, NH, 1), csum.dtype), csum], axis=-1)
            lfm = csum[:, :, :, None] - csum[:, :, None, :]
            ltr = jnp.tril(jnp.ones((Sq, Sq), dtype=bool))
            log_fg_matrix = jnp.where(ltr, lfm[:, :, 1:, 1:], -jnp.inf)
            log_D = log_fg_matrix + ig[:, :, None, :]
            max_log_D = jnp.max(log_D, axis=-1, keepdims=True)
            D = jnp.exp(log_D - max_log_D)
            k_scaled = kh / np.sqrt(DH).astype(np.float32)
            pe = pos_emb.reshape(Sq, Sq, NH, DH)
            k_hop = jnp.einsum('bhvc,vmhc->bhvm', qh, pe)
            qk = jnp.einsum('bhsd,bhtd->bhst', qh, k_scaled)
            C = (qk + k_hop) * D
            normalizer = jnp.maximum(jnp.abs(jnp.sum(C, axis=-1, keepdims=True)), jnp.exp(-max_log_D))
            Cn = C / (normalizer + EPS)
            h = Cn @ vh
            mu = jnp.mean(h, axis=-1, keepdims=True)
            var = jnp.mean(jnp.square(h - mu), axis=-1, keepdims=True)
            hn = (h - mu) / jnp.sqrt(var + LN_EPS)
            w = (1.0 + ln_w).reshape(NH, DH)
            b = ln_b.reshape(NH, DH)
            hn = hn * w[None, :, None, :] + b[None, :, None, :]
            return hn.transpose(0, 2, 1, 3).reshape(Bq, Sq, DIM)
        key = jax.random.key(seed)
        ks = jax.random.split(key, 8)
        hops_np, curnum = _make_hops(S)
        return {'q': jax.random.normal(ks[0], (B, S, DIM), dtype=jnp.float32), 'k': jax.random.normal(ks[1], (B, S, DIM), dtype=jnp.float32), 'v': jax.random.normal(ks[2], (B, S, DIM), dtype=jnp.float32), 'igate_w': jax.random.normal(ks[3], (NH, 3 * DIM), dtype=jnp.float32) * 0.02, 'igate_b': jax.random.normal(ks[4], (NH,), dtype=jnp.float32) * 0.1, 'fgate_w': jax.random.normal(ks[5], (NH, 3 * DIM), dtype=jnp.float32) * 0.02, 'fgate_b': jnp.linspace(3.0, 6.0, NH, dtype=jnp.float32), 'rpe': jax.random.normal(ks[6], (curnum, DIM), dtype=jnp.float32) * 0.02, 'ln_w': jax.random.normal(ks[7], (DIM,), dtype=jnp.float32) * 0.1, 'ln_b': jnp.zeros((DIM,), dtype=jnp.float32), 'hops': jnp.asarray(hops_np)}
    _L0_xattn_all = _L0_xattn_setup()
    _L0_xattn_in = {k: v for k, v in _L0_xattn_all.items() if k in ('igate_w', 'igate_b', 'fgate_w', 'fgate_b', 'rpe', 'ln_w', 'ln_b')}
    del _L0_xattn_all

    def _L0_ffn_setup():
        import jax, jax.numpy as jnp
        import numpy as np
        B, T, C, H, E, K = (4, 256, 256, 256, 8, 2)

        def _swiglu(x):
            a, b = jnp.split(x, 2, axis=-1)
            return jax.nn.silu(a) * b
        key = jax.random.key(seed)
        ks = jax.random.split(key, 6)
        s = 0.02
        x = jax.random.normal(ks[0], (B, T, C), jnp.float32)
        w_shared_in = jax.random.normal(ks[1], (C, 2 * H), jnp.float32) * s
        w_shared_out = jax.random.normal(ks[2], (H, C), jnp.float32) * s
        w1_shared = jax.random.normal(ks[3], (C, 2 * H), jnp.float32) * s
        w2 = jax.random.normal(ks[4], (E, H, C), jnp.float32) * s
        w_gate = jax.random.normal(ks[5], (C, E), jnp.float32) * s
        gate_bias = jnp.zeros((E,), jnp.float32)
        return {'x': x, 'w_shared_in': w_shared_in, 'w_shared_out': w_shared_out, 'w1_shared': w1_shared, 'w2': w2, 'w_gate': w_gate, 'gate_bias': gate_bias}
    _L0_ffn_all = _L0_ffn_setup()
    _L0_ffn_in = {k: v for k, v in _L0_ffn_all.items() if k in ('w_shared_in', 'w_shared_out', 'w1_shared', 'w2', 'w_gate', 'gate_bias')}
    del _L0_ffn_all

    def _L1_xattn_setup():
        import jax, jax.numpy as jnp
        import numpy as np
        N_HEAD = 16
        key = jax.random.key(seed)
        ks = jax.random.split(key, 5)
        b, l, d = (4, 512, 256)
        dh = d // N_HEAD
        return {'q': jax.random.normal(ks[0], (b, l, d), dtype=jnp.float32), 'kv': jax.random.normal(ks[1], (b, l, d), dtype=jnp.float32), 'Wq': jax.random.normal(ks[2], (d, d), dtype=jnp.float32) * 0.02, 'Wkv': jax.random.normal(ks[3], (2 * dh, d), dtype=jnp.float32) * 0.02, 'Wc': jax.random.normal(ks[4], (d, d), dtype=jnp.float32) * 0.02}
    _L1_xattn_all = _L1_xattn_setup()
    _L1_xattn_in = {k: v for k, v in _L1_xattn_all.items() if k in ('Wq', 'Wkv', 'Wc')}
    del _L1_xattn_all

    def _L1_ffn_setup():
        import math
        import jax, jax.numpy as jnp
        import numpy as np
        E = 8
        H = 256
        HP = 128
        SPARSITY = 8
        N_ROTATE = 64
        ROPE_BASE = 10000.0

        def _rope(x, pos):
            half = N_ROTATE // 2
            inv_freq = 1.0 / ROPE_BASE ** (jnp.arange(half, dtype=jnp.float32) * 2.0 / N_ROTATE)
            ang = pos.astype(jnp.float32)[..., None] * inv_freq
            sin, cos = (jnp.sin(ang), jnp.cos(ang))
            x1, x2 = (x[..., :half], x[..., half:])
            return jnp.concatenate([x1 * cos - x2 * sin, x2 * cos + x1 * sin], axis=-1)
        key = jax.random.key(seed)
        k1, k2, k3, k4 = jax.random.split(key, 4)
        B, T = (4, 2048)
        X = jax.random.normal(k1, (B, T, H), dtype=jnp.float32)
        Wr = jax.random.uniform(k2, (E, H), minval=-1 / math.sqrt(H), maxval=1 / math.sqrt(H), dtype=jnp.float32)
        bq = 1 / math.sqrt(3 * HP)
        Wqkv = jax.random.uniform(k3, (E, H, 3 * HP), minval=-bq, maxval=bq, dtype=jnp.float32)
        bo = 1 / math.sqrt(H * E)
        Wo = jax.random.uniform(k4, (E, HP, H), minval=-bo, maxval=bo, dtype=jnp.float32)
        return {'X': X, 'Wr': Wr, 'Wqkv': Wqkv, 'Wo': Wo}
    _L1_ffn_all = _L1_ffn_setup()
    _L1_ffn_in = {k: v for k, v in _L1_ffn_all.items() if k in ('Wr', 'Wqkv', 'Wo')}
    del _L1_ffn_all

    def _L2_xattn_setup():
        import jax, jax.numpy as jnp
        import numpy as np
        D_MODEL = 256
        N_HEAD = 16
        HEAD_DIM = D_MODEL // N_HEAD
        key = jax.random.key(seed)
        ks = jax.random.split(key, 9)
        B, T = (2, 512)
        s = 0.02
        return {'k': jax.random.normal(ks[0], (B, T, D_MODEL), jnp.float32), 'q': jax.random.normal(ks[1], (B, T, D_MODEL), jnp.float32), 'v': jax.random.normal(ks[2], (B, T, D_MODEL), jnp.float32), 'Wk': jax.random.normal(ks[3], (D_MODEL, D_MODEL), jnp.float32) * s, 'bk': jnp.zeros((D_MODEL,), jnp.float32), 'Wq': jax.random.normal(ks[4], (D_MODEL, D_MODEL), jnp.float32) * s, 'bq': jnp.zeros((D_MODEL,), jnp.float32), 'Wc': jax.random.normal(ks[5], (D_MODEL, D_MODEL), jnp.float32) * s, 'bc': jnp.zeros((D_MODEL,), jnp.float32)}
    _L2_xattn_all = _L2_xattn_setup()
    _L2_xattn_in = {k: v for k, v in _L2_xattn_all.items() if k in ('Wk', 'bk', 'Wq', 'bq', 'Wc', 'bc')}
    del _L2_xattn_all

    def _L2_ffn_setup():
        import jax, jax.numpy as jnp
        import numpy as np
        E = 16
        K = 2
        LOAD = 1.0

        def _dispatch(xb, pb, cap):
            T, C = xb.shape
            top_k_probs, ei = jax.lax.top_k(pb, K)
            flat = ei.swapaxes(0, 1).ravel()
            one_hot = jax.nn.one_hot(flat, E, dtype=jnp.int32)
            pos = jnp.cumsum(one_hot, axis=0) * one_hot
            pos = pos.reshape(K, T, E).swapaxes(0, 1)
            pos = jnp.max(pos, axis=-1) - 1
            ei2 = flat.reshape(K, T).swapaxes(0, 1)
            xr = jnp.repeat(xb, K, axis=0)
            buf = jnp.zeros((E, cap, C), xb.dtype)
            buf = buf.at[ei2.ravel(), pos.ravel()].set(xr, mode='drop')
            return (top_k_probs, pos, ei2, buf)

        def _collect(eo_b, ei_b, pos_b, tk_b):
            out = eo_b[ei_b, pos_b]
            return jnp.sum(tk_b[..., None] * out, axis=1)
        key = jax.random.key(seed)
        k1, k2, k3, k4, k5 = jax.random.split(key, 5)
        B, T, C, H = (8, 1024, 256, 128)
        n_layer = 12
        x = jax.random.normal(k1, (B, T, C), dtype=jnp.float32)
        w_router = jax.random.normal(k2, (C, E), dtype=jnp.float32) * 0.02
        w_fc = jax.random.normal(k3, (E, C, H), dtype=jnp.float32) * 0.02
        w_gate = jax.random.normal(k4, (E, C, H), dtype=jnp.float32) * 0.02
        w_proj = jax.random.normal(k5, (E, H, C), dtype=jnp.float32) * (0.02 * (2 * n_layer) ** (-0.5))
        return {'x': x, 'w_router': w_router, 'w_fc': w_fc, 'w_gate': w_gate, 'w_proj': w_proj}
    _L2_ffn_all = _L2_ffn_setup()
    _L2_ffn_in = {k: v for k, v in _L2_ffn_all.items() if k in ('w_router', 'w_fc', 'w_gate', 'w_proj')}
    del _L2_ffn_all

    def _L3_xattn_setup():
        import jax, jax.numpy as jnp
        import numpy as np
        EMBED_DIM = 256
        NUM_HEADS = 16
        HEAD_DIM = EMBED_DIM // NUM_HEADS
        SCALE = HEAD_DIM ** (-0.5)
        key = jax.random.key(seed)
        ks = jax.random.split(key, 8)
        B, Nq, Nkv, C = (2, 512, 512, EMBED_DIM)
        s = C ** (-0.5)
        return {'q': jax.random.normal(ks[0], (B, Nq, C), dtype=jnp.float32), 'kv': jax.random.normal(ks[1], (B, Nkv, C), dtype=jnp.float32), 'w_q': jax.random.normal(ks[2], (C, C), dtype=jnp.float32) * s, 'b_q': jnp.zeros((C,), dtype=jnp.float32), 'w_kv': jax.random.normal(ks[3], (C, 2 * C), dtype=jnp.float32) * s, 'b_kv': jnp.zeros((2 * C,), dtype=jnp.float32), 'w_out': jax.random.normal(ks[4], (C, C), dtype=jnp.float32) * s, 'b_out': jnp.zeros((C,), dtype=jnp.float32)}
    _L3_xattn_all = _L3_xattn_setup()
    _L3_xattn_in = {k: v for k, v in _L3_xattn_all.items() if k in ('w_q', 'b_q', 'w_kv', 'b_kv', 'w_out', 'b_out')}
    del _L3_xattn_all

    def _L3_ffn_setup():
        import jax, jax.numpy as jnp
        import numpy as np
        EMB = 256
        HID = 256
        E = 16
        K = 2
        key = jax.random.key(seed)
        ks = jax.random.split(key, 5)
        s_in = (2.0 / EMB) ** 0.5
        s_hid = (2.0 / HID) ** 0.5
        x = jax.random.normal(ks[0], (2, 1024, EMB), dtype=jnp.float32)
        w_gate = jax.random.normal(ks[1], (EMB, E), dtype=jnp.float32) * s_in
        w1 = jax.random.normal(ks[2], (E, EMB, HID), dtype=jnp.float32) * s_in
        w2 = jax.random.normal(ks[3], (E, EMB, HID), dtype=jnp.float32) * s_in
        wc = jax.random.normal(ks[4], (E, HID, EMB), dtype=jnp.float32) * s_hid
        return {'x': x, 'w_gate': w_gate, 'w1': w1, 'w2': w2, 'wc': wc}
    _L3_ffn_all = _L3_ffn_setup()
    _L3_ffn_in = {k: v for k, v in _L3_ffn_all.items() if k in ('w_gate', 'w1', 'w2', 'wc')}
    del _L3_ffn_all
    return {'x': x, 'ctx_1024': ctx_1024, 'itok_SxS2_0_2016': itok_SxS2_0_2016, 'L0_xattn_igate_w': _L0_xattn_in['igate_w'], 'L0_xattn_igate_b': _L0_xattn_in['igate_b'], 'L0_xattn_fgate_w': _L0_xattn_in['fgate_w'], 'L0_xattn_fgate_b': _L0_xattn_in['fgate_b'], 'L0_xattn_rpe': _L0_xattn_in['rpe'], 'L0_xattn_ln_w': _L0_xattn_in['ln_w'], 'L0_xattn_ln_b': _L0_xattn_in['ln_b'], 'L0_ffn_w_shared_in': _L0_ffn_in['w_shared_in'], 'L0_ffn_w_shared_out': _L0_ffn_in['w_shared_out'], 'L0_ffn_w1_shared': _L0_ffn_in['w1_shared'], 'L0_ffn_w2': _L0_ffn_in['w2'], 'L0_ffn_w_gate': _L0_ffn_in['w_gate'], 'L0_ffn_gate_bias': _L0_ffn_in['gate_bias'], 'L1_xattn_Wq': _L1_xattn_in['Wq'], 'L1_xattn_Wkv': _L1_xattn_in['Wkv'], 'L1_xattn_Wc': _L1_xattn_in['Wc'], 'L1_ffn_Wr': _L1_ffn_in['Wr'], 'L1_ffn_Wqkv': _L1_ffn_in['Wqkv'], 'L1_ffn_Wo': _L1_ffn_in['Wo'], 'L2_xattn_Wk': _L2_xattn_in['Wk'], 'L2_xattn_bk': _L2_xattn_in['bk'], 'L2_xattn_Wq': _L2_xattn_in['Wq'], 'L2_xattn_bq': _L2_xattn_in['bq'], 'L2_xattn_Wc': _L2_xattn_in['Wc'], 'L2_xattn_bc': _L2_xattn_in['bc'], 'L2_ffn_w_router': _L2_ffn_in['w_router'], 'L2_ffn_w_fc': _L2_ffn_in['w_fc'], 'L2_ffn_w_gate': _L2_ffn_in['w_gate'], 'L2_ffn_w_proj': _L2_ffn_in['w_proj'], 'L3_xattn_w_q': _L3_xattn_in['w_q'], 'L3_xattn_b_q': _L3_xattn_in['b_q'], 'L3_xattn_w_kv': _L3_xattn_in['w_kv'], 'L3_xattn_b_kv': _L3_xattn_in['b_kv'], 'L3_xattn_w_out': _L3_xattn_in['w_out'], 'L3_xattn_b_out': _L3_xattn_in['b_out'], 'L3_ffn_w_gate': _L3_ffn_in['w_gate'], 'L3_ffn_w1': _L3_ffn_in['w1'], 'L3_ffn_w2': _L3_ffn_in['w2'], 'L3_ffn_wc': _L3_ffn_in['wc']}

def reference(x, ctx_1024, itok_SxS2_0_2016, L0_xattn_igate_w, L0_xattn_igate_b, L0_xattn_fgate_w, L0_xattn_fgate_b, L0_xattn_rpe, L0_xattn_ln_w, L0_xattn_ln_b, L0_ffn_w_shared_in, L0_ffn_w_shared_out, L0_ffn_w1_shared, L0_ffn_w2, L0_ffn_w_gate, L0_ffn_gate_bias, L1_xattn_Wq, L1_xattn_Wkv, L1_xattn_Wc, L1_ffn_Wr, L1_ffn_Wqkv, L1_ffn_Wo, L2_xattn_Wk, L2_xattn_bk, L2_xattn_Wq, L2_xattn_bq, L2_xattn_Wc, L2_xattn_bc, L2_ffn_w_router, L2_ffn_w_fc, L2_ffn_w_gate, L2_ffn_w_proj, L3_xattn_w_q, L3_xattn_b_q, L3_xattn_w_kv, L3_xattn_b_kv, L3_xattn_w_out, L3_xattn_b_out, L3_ffn_w_gate, L3_ffn_w1, L3_ffn_w2, L3_ffn_wc):
    import jax
    import jax.numpy as jnp

    def _L0_xattn_ref(q, k, v, igate_w, igate_b, fgate_w, fgate_b, rpe, ln_w, ln_b, hops):
        import jax, jax.numpy as jnp
        import numpy as np
        B, S, DIM, NH = (64, 64, 256, 8)
        DH = DIM // NH
        EPS = 1e-06
        LN_EPS = 1e-05

        def _make_hops(n):
            hops = np.zeros((n, n), dtype=np.int64)
            cur = 1
            for i in range(n):
                for j in range(i + 1, n):
                    hops[i, j] = cur
                    hops[j, i] = cur
                    cur += 1
            return (hops, cur)

        def _mlstm_forward(q, k, v, igate_w, igate_b, fgate_w, fgate_b, rpe, ln_w, ln_b, hops):
            Bq, Sq, _ = q.shape
            pos_emb = rpe[hops]
            gate_in = jnp.concatenate([q, k, v], axis=-1)
            ig = gate_in @ igate_w.T + igate_b
            fg = gate_in @ fgate_w.T + fgate_b
            ig = jnp.transpose(ig, (0, 2, 1))
            fg = jnp.transpose(fg, (0, 2, 1))
            qh = q.reshape(Bq, Sq, NH, DH).transpose(0, 2, 1, 3)
            kh = k.reshape(Bq, Sq, NH, DH).transpose(0, 2, 1, 3)
            vh = v.reshape(Bq, Sq, NH, DH).transpose(0, 2, 1, 3)
            log_f = jax.nn.log_sigmoid(fg)
            csum = jnp.cumsum(log_f, axis=-1)
            csum = jnp.concatenate([jnp.zeros((Bq, NH, 1), csum.dtype), csum], axis=-1)
            lfm = csum[:, :, :, None] - csum[:, :, None, :]
            ltr = jnp.tril(jnp.ones((Sq, Sq), dtype=bool))
            log_fg_matrix = jnp.where(ltr, lfm[:, :, 1:, 1:], -jnp.inf)
            log_D = log_fg_matrix + ig[:, :, None, :]
            max_log_D = jnp.max(log_D, axis=-1, keepdims=True)
            D = jnp.exp(log_D - max_log_D)
            k_scaled = kh / np.sqrt(DH).astype(np.float32)
            pe = pos_emb.reshape(Sq, Sq, NH, DH)
            k_hop = jnp.einsum('bhvc,vmhc->bhvm', qh, pe)
            qk = jnp.einsum('bhsd,bhtd->bhst', qh, k_scaled)
            C = (qk + k_hop) * D
            normalizer = jnp.maximum(jnp.abs(jnp.sum(C, axis=-1, keepdims=True)), jnp.exp(-max_log_D))
            Cn = C / (normalizer + EPS)
            h = Cn @ vh
            mu = jnp.mean(h, axis=-1, keepdims=True)
            var = jnp.mean(jnp.square(h - mu), axis=-1, keepdims=True)
            hn = (h - mu) / jnp.sqrt(var + LN_EPS)
            w = (1.0 + ln_w).reshape(NH, DH)
            b = ln_b.reshape(NH, DH)
            hn = hn * w[None, :, None, :] + b[None, :, None, :]
            return hn.transpose(0, 2, 1, 3).reshape(Bq, Sq, DIM)
        return _mlstm_forward(q, k, v, igate_w, igate_b, fgate_w, fgate_b, rpe, ln_w, ln_b, hops)

    def _L0_ffn_ref(x, w_shared_in, w_shared_out, w1_shared, w2, w_gate, gate_bias):
        import jax, jax.numpy as jnp
        import numpy as np
        B, T, C, H, E, K = (4, 256, 256, 256, 8, 2)

        def _swiglu(x):
            a, b = jnp.split(x, 2, axis=-1)
            return jax.nn.silu(a) * b
        Bx, Tx, Cx = x.shape
        S = Bx * Tx
        fx = x.reshape(S, Cx)
        shared_out = _swiglu(fx @ w_shared_in) @ w_shared_out
        logits = fx @ w_gate + gate_bias
        probs = jax.nn.softmax(logits, axis=-1)
        top_val, top_idx = jax.lax.top_k(probs, K)
        wdense = jnp.zeros((S, E), probs.dtype).at[jnp.arange(S)[:, None], top_idx].add(top_val)
        hid = _swiglu(fx @ w1_shared)
        routed_out = jnp.zeros_like(shared_out)
        for e in range(E):
            routed_out = routed_out + wdense[:, e:e + 1] * (hid @ w2[e])
        return (shared_out + routed_out).reshape(Bx, Tx, Cx)

    def _L1_xattn_ref(q, kv, Wq, Wkv, Wc):
        import jax, jax.numpy as jnp
        import numpy as np
        N_HEAD = 16
        b, l, d = q.shape
        h = N_HEAD
        dh = d // h
        qp = jnp.einsum('bld,ed->ble', q, Wq)
        scores = jnp.einsum('bld,bmd->blm', qp, kv)
        idx = jnp.argmax(scores, axis=-1)
        mem = jnp.take_along_axis(kv, idx[..., None], axis=1)
        mkv = jnp.einsum('bld,ed->ble', mem, Wkv)
        mk, mv = jnp.split(mkv, 2, axis=-1)
        qh = qp.reshape(b, l, h, dh).transpose(0, 2, 1, 3)
        scale = 1.0 / np.sqrt(dh).astype(np.float32)
        logits = jnp.einsum('bhld,bmd->bhlm', qh, mk) * scale
        attn = jax.nn.softmax(logits, axis=-1)
        out = jnp.einsum('bhlm,bmd->bhld', attn, mv)
        out = out.transpose(0, 2, 1, 3).reshape(b, l, d)
        return jnp.einsum('bld,ed->ble', out, Wc)

    def _L1_ffn_ref(X, Wr, Wqkv, Wo):
        import math
        import jax, jax.numpy as jnp
        import numpy as np
        E = 8
        H = 256
        HP = 128
        SPARSITY = 8
        N_ROTATE = 64
        ROPE_BASE = 10000.0

        def _rope(x, pos):
            half = N_ROTATE // 2
            inv_freq = 1.0 / ROPE_BASE ** (jnp.arange(half, dtype=jnp.float32) * 2.0 / N_ROTATE)
            ang = pos.astype(jnp.float32)[..., None] * inv_freq
            sin, cos = (jnp.sin(ang), jnp.cos(ang))
            x1, x2 = (x[..., :half], x[..., half:])
            return jnp.concatenate([x1 * cos - x2 * sin, x2 * cos + x1 * sin], axis=-1)
        B, T, _ = X.shape
        k = min(max(T // SPARSITY, 2), T)
        logits = jax.nn.sigmoid(jnp.einsum('bth,eh->bte', X, Wr))
        topk_vals, topk_I = jax.lax.top_k(logits.transpose(0, 2, 1), k)
        idx_flat = topk_I.reshape(B, E * k)
        Xg = jnp.take_along_axis(X, idx_flat[:, :, None], axis=1).reshape(B, E, k, H)
        QKV = jnp.einsum('beki,eij->bekj', Xg, Wqkv)
        Q, K, V = jnp.split(QKV, 3, axis=-1)
        Q = jnp.concatenate([_rope(Q[..., :N_ROTATE], topk_I), Q[..., N_ROTATE:]], axis=-1)
        K = jnp.concatenate([_rope(K[..., :N_ROTATE], topk_I), K[..., N_ROTATE:]], axis=-1)
        M = topk_I[..., :, None] >= topk_I[..., None, :]
        scores = jnp.einsum('bekd,bemd->bekm', Q, K) / math.sqrt(HP)
        scores = jnp.where(M, scores, -jnp.inf)
        A = jax.nn.softmax(scores, axis=-1)
        AV = jnp.einsum('bekm,bemd->bekd', A, V)
        AV = AV * topk_vals[..., None]
        Xpre = jnp.einsum('bekj,eji->beki', AV, Wo)
        out = jnp.zeros((B, T, H), dtype=X.dtype)
        out = out.at[jnp.arange(B)[:, None], idx_flat].add(Xpre.reshape(B, E * k, H))
        return out

    def _L2_xattn_ref(k, q, v, Wk, bk, Wq, bq, Wc, bc):
        import jax, jax.numpy as jnp
        import numpy as np
        D_MODEL = 256
        N_HEAD = 16
        HEAD_DIM = D_MODEL // N_HEAD
        B, T_v, C = v.shape
        T_q = q.shape[1]
        H, hd = (N_HEAD, C // N_HEAD)
        kp = k @ Wk.T + bk
        qp = q @ Wq.T + bq
        kh = kp.reshape(B, T_v, H, hd).transpose(0, 2, 1, 3)
        qh = qp.reshape(B, T_q, H, hd).transpose(0, 2, 1, 3)
        vh = v.reshape(B, T_v, H, hd).transpose(0, 2, 1, 3)
        scale = 1.0 / jnp.sqrt(jnp.asarray(hd, kh.dtype))
        att = jnp.einsum('bhqd,bhkd->bhqk', qh, kh) * scale
        att = jax.nn.softmax(att, axis=-1)
        y = jnp.einsum('bhqk,bhkd->bhqd', att, vh)
        y = y.transpose(0, 2, 1, 3).reshape(B, T_q, C)
        return y @ Wc.T + bc

    def _L2_ffn_ref(x, w_router, w_fc, w_gate, w_proj):
        import jax, jax.numpy as jnp
        import numpy as np
        E = 16
        K = 2
        LOAD = 1.0

        def _dispatch(xb, pb, cap):
            T, C = xb.shape
            top_k_probs, ei = jax.lax.top_k(pb, K)
            flat = ei.swapaxes(0, 1).ravel()
            one_hot = jax.nn.one_hot(flat, E, dtype=jnp.int32)
            pos = jnp.cumsum(one_hot, axis=0) * one_hot
            pos = pos.reshape(K, T, E).swapaxes(0, 1)
            pos = jnp.max(pos, axis=-1) - 1
            ei2 = flat.reshape(K, T).swapaxes(0, 1)
            xr = jnp.repeat(xb, K, axis=0)
            buf = jnp.zeros((E, cap, C), xb.dtype)
            buf = buf.at[ei2.ravel(), pos.ravel()].set(xr, mode='drop')
            return (top_k_probs, pos, ei2, buf)

        def _collect(eo_b, ei_b, pos_b, tk_b):
            out = eo_b[ei_b, pos_b]
            return jnp.sum(tk_b[..., None] * out, axis=1)
        B, T, C = x.shape
        cap = int(LOAD * K * max(1, T / E))
        g = jnp.einsum('btc,ce->bte', x, w_router)
        gate_probs = jax.nn.softmax(g, axis=-1)
        top_k_probs, positions, indices, expert_inputs = jax.vmap(lambda xb, pb: _dispatch(xb, pb, cap))(x, gate_probs)
        expert_inputs = jnp.swapaxes(expert_inputs, 0, 1).reshape(E, B * cap, C)
        gg = jnp.einsum('enc,ech->enh', expert_inputs, w_gate)
        h = jnp.einsum('enc,ech->enh', expert_inputs, w_fc)
        h = jax.nn.silu(gg) * h
        o = jnp.einsum('enh,ehc->enc', h, w_proj)
        expert_outputs = jnp.swapaxes(o.reshape(E, B, cap, C), 0, 1)
        y = jax.vmap(_collect)(expert_outputs, indices, positions, top_k_probs)
        return y

    def _L3_xattn_ref(q, kv, w_q, b_q, w_kv, b_kv, w_out, b_out):
        import jax, jax.numpy as jnp
        import numpy as np
        EMBED_DIM = 256
        NUM_HEADS = 16
        HEAD_DIM = EMBED_DIM // NUM_HEADS
        SCALE = HEAD_DIM ** (-0.5)
        B, Nq, C = q.shape
        _, Nkv, _ = kv.shape
        H, D = (NUM_HEADS, HEAD_DIM)
        qp = (q @ w_q + b_q).reshape(B, Nq, H, D).transpose(0, 2, 1, 3)
        kvp = (kv @ w_kv + b_kv).reshape(B, Nkv, 2, H, D).transpose(2, 0, 3, 1, 4)
        kp, vp = (kvp[0], kvp[1])
        attn = jnp.einsum('bhqd,bhkd->bhqk', qp, kp) * SCALE
        attn = jax.nn.softmax(attn, axis=-1)
        out = jnp.einsum('bhqk,bhkd->bhqd', attn, vp)
        out = out.transpose(0, 2, 1, 3).reshape(B, Nq, C)
        return out @ w_out + b_out

    def _L3_ffn_ref(x, w_gate, w1, w2, wc):
        import jax, jax.numpy as jnp
        import numpy as np
        EMB = 256
        HID = 256
        E = 16
        K = 2
        b, s, d = x.shape
        xf = x.reshape(-1, d)
        n = xf.shape[0]
        probs = jax.nn.softmax(xf @ w_gate, axis=-1)
        scores, idx = jax.lax.top_k(probs, K)
        gates = jnp.zeros((n, E), dtype=xf.dtype).at[jnp.arange(n)[:, None], idx].set(scores)

        def body(acc, ws):
            w1e, w2e, wce, ge = ws
            h = jax.nn.silu(xf @ w1e) * (xf @ w2e)
            return (acc + ge[:, None] * (h @ wce), None)
        out, _ = jax.lax.scan(body, jnp.zeros_like(xf), (w1, w2, wc, gates.T))
        return out.reshape(b, s, d)
    x = x + _L0_xattn_ref(_layernorm(x, axis=-1), ctx_1024, ctx_1024, L0_xattn_igate_w, L0_xattn_igate_b, L0_xattn_fgate_w, L0_xattn_fgate_b, L0_xattn_rpe, L0_xattn_ln_w, L0_xattn_ln_b, itok_SxS2_0_2016)
    x = x + _L0_ffn_ref(_layernorm(x, axis=-1), L0_ffn_w_shared_in, L0_ffn_w_shared_out, L0_ffn_w1_shared, L0_ffn_w2, L0_ffn_w_gate, L0_ffn_gate_bias)
    x = x + _L1_xattn_ref(_layernorm(x, axis=-1), ctx_1024, L1_xattn_Wq, L1_xattn_Wkv, L1_xattn_Wc)
    x = x + _L1_ffn_ref(_layernorm(x, axis=-1), L1_ffn_Wr, L1_ffn_Wqkv, L1_ffn_Wo)
    x = x + _L2_xattn_ref(ctx_1024, _layernorm(x, axis=-1), ctx_1024, L2_xattn_Wk, L2_xattn_bk, L2_xattn_Wq, L2_xattn_bq, L2_xattn_Wc, L2_xattn_bc)
    x = x + _L2_ffn_ref(_layernorm(x, axis=-1), L2_ffn_w_router, L2_ffn_w_fc, L2_ffn_w_gate, L2_ffn_w_proj)
    x = x + _L3_xattn_ref(_layernorm(x, axis=-1), ctx_1024, L3_xattn_w_q, L3_xattn_b_q, L3_xattn_w_kv, L3_xattn_b_kv, L3_xattn_w_out, L3_xattn_b_out)
    x = x + _L3_ffn_ref(_layernorm(x, axis=-1), L3_ffn_w_gate, L3_ffn_w1, L3_ffn_w2, L3_ffn_wc)
    return x

_drawn_inputs = setup_inputs


def setup_inputs(seed=0):
    import zlib

    import numpy as np

    out = dict(_drawn_inputs(seed))
    spreads = {'L0_xattn_ln_b': (0.0, 0.1),
     'L0_ffn_gate_bias': (0.0, 0.8),
     'L2_xattn_bk': (0.0, 2.0),
     'L2_xattn_bq': (0.0, 0.8),
     'L2_xattn_bc': (0.0, 0.1),
     'L3_xattn_b_q': (0.0, 1.369),
     'L3_xattn_b_kv': (0.0, 0.315),
     'L3_xattn_b_out': (0.0, 0.296)}
    factors = {'L0_xattn_igate_b': 64.0,
     'L0_ffn_w1_shared': 6.807,
     'L0_ffn_w2': 5.933,
     'L0_ffn_w_gate': 6.792,
     'L1_xattn_Wq': 9.495,
     'L1_ffn_Wqkv': 2.669,
     'L1_ffn_Wo': 2.761,
     'L2_xattn_Wk': 4.989,
     'L2_xattn_Wq': 5.39,
     'L2_ffn_w_router': 8.0,
     'L2_ffn_w_fc': 8.0,
     'L2_ffn_w_gate': 8.0,
     'L2_ffn_w_proj': 8.0,
     'L0_ffn_w_shared_in': 2.964,
     'L0_ffn_w_shared_out': 3.363}
    for name, (base, spread) in spreads.items():
        noise = np.random.default_rng([zlib.crc32(name.encode()), seed]).standard_normal(out[name].shape)
        drawn = base * np.exp(spread * noise) if base else spread * noise
        out[name] = jnp.asarray(drawn.astype(out[name].dtype))
    for name, factor in factors.items():
        out[name] = (out[name] * factor).astype(out[name].dtype)
    return out
```

```python
from contextlib import ExitStack

import concourse.bass as bass
from concourse import mybir

P = 128
B, S, D = 8, 256, 256
TT = S // P
KD = D // P
F32 = mybir.dt.float32
BF16 = mybir.dt.bfloat16
I32 = mybir.dt.int32
U32 = mybir.dt.uint32
ALU = mybir.AluOpType
ACT = mybir.ActivationFunctionType
AX = mybir.AxisListType
LN_EPS = 1e-5
MADE = 5


class Steps:

    def __init__(self, eng, sem, before, planned):
        self.eng, self.sem, self.before, self.planned, self.n = eng, sem, before, planned, 0

    def step(self, instruction, apart=None):
        self.n += 1
        instruction.then_inc(self.sem, 1)
        self.eng.wait_ge(self.sem, self.before + self.n)
        if apart is not None:
            self.eng.sem_inc(apart, 1)

    def end(self):
        assert self.n == self.planned, (self.sem, self.n)


def wait_apart(eng, sem, value, apart):
    eng.wait_ge(sem, value)
    eng.sem_inc(apart, 1)


def bc(ap, shape):
    return ap.to_broadcast(shape)


def layer_norm(dve, steps, x, tok, work, out, ready, apart):
    stats, mv, ve, y, u = work
    for t in range(TT):
        steps.step(dve.bn_stats(stats[:, t, :], x[:, tok + t, :]), apart)
    for t in range(TT):
        steps.step(dve.bn_aggr(mv[:, t, :], stats[:, t, :]), apart)
    steps.step(dve.tensor_scalar(ve[:, :], mv[:, :, 1], LN_EPS, None, ALU.add))
    rsqrt(steps, dve, ve[:, :], y[:, :], u[:, :])
    for t in range(TT):
        last = dve.tensor_scalar(out[:, t, :], x[:, tok + t, :], mv[:, t, 0:1], y[:, t:t + 1],
                                 ALU.subtract, ALU.mult)
    last.then_inc(ready, 1)


def rsqrt(steps, dve, ve, y, u):
    steps.step(dve.tensor_scalar(y.bitcast(I32), ve.bitcast(I32), 1, None, ALU.arith_shift_right))
    steps.step(dve.tensor_scalar(y.bitcast(I32), y.bitcast(I32), -1.0, float(0x5F3759DF), ALU.mult, ALU.add))
    for _ in range(3):
        steps.step(dve.tensor_tensor(u, y, y, ALU.mult))
        steps.step(dve.tensor_tensor(u, u, ve, ALU.mult))
        steps.step(dve.tensor_scalar(u, u, -0.5, 1.5, ALU.mult, ALU.add))
        steps.step(dve.tensor_tensor(y, y, u, ALU.mult))


LN_STEPS = 2 * TT + 1 + 2 + 12


def ln_work(sb, tag):
    return (sb(f"{tag}_stats", [P, TT, 6]), sb(f"{tag}_mv", [P, TT, 2]), sb(f"{tag}_ve", [P, TT]),
            sb(f"{tag}_rstd", [P, TT]), sb(f"{tag}_u", [P, TT]))


def turn_tokens(pe, ps, xn, ident):
    for k in range(KD):
        for t in range(TT):
            last = pe.transpose(ps[:, k * S + t * P:k * S + t * P + P], xn[:, t, k * P:(k + 1) * P], ident[:, :])
    return last


def route(dve, steps, E, logits, bias, work, iota, z_ready, exp_ready, turn, apart, chosen=None):
    lg, mx, ez, rs, top, ix, ixf, oh = work
    if bias is None:
        steps.step(dve.tensor_copy(lg[:, :, :], logits))
    else:
        steps.step(dve.tensor_tensor(lg[:, :, :], logits, bias, ALU.add))
    steps.step(dve.tensor_reduce(mx[:, :], lg[:, :, :], AX.X, ALU.max))
    steps.step(dve.tensor_tensor(lg[:, :, :], lg[:, :, :], bc(mx[:, :, None], [P, TT, E]), ALU.subtract))
    dve.tensor_scalar(lg[:, :, :], lg[:, :, :], -104.0, None, ALU.max).then_inc(z_ready, 1)
    dve.wait_ge(z_ready, turn + 1)
    dve.sem_inc(apart, 1)
    for t in range(TT):
        steps.step(dve.max(top[:, t, :], lg[:, t, :]), apart)
    for t in range(TT):
        steps.step(dve.max_index(ix[:, t, :], top[:, t, :], lg[:, t, :]), apart)
    steps.step(dve.tensor_copy(ixf[:, :, :], ix[:, :, :]))
    for k in range(2):
        steps.step(dve.tensor_tensor(oh[:, k, :, :], bc(iota[:, None, 0:E], [P, TT, E]),
                                     bc(ixf[:, :, k:k + 1], [P, TT, E]), ALU.is_equal))
    if chosen is not None:
        dve.sem_inc(chosen, 1)
    dve.wait_ge(exp_ready, turn + 1)
    steps.step(dve.tensor_reduce(rs[:, :], ez[:, :, :], AX.X, ALU.add))
    steps.step(dve.reciprocal(rs[:, :], rs[:, :]))
    steps.step(dve.tensor_tensor(ez[:, :, :], ez[:, :, :], bc(rs[:, :, None], [P, TT, E]), ALU.mult))


ROUTE_STEPS = 3 + 4 + 1 + 2 + 3


def route_work(sb, tag, E):
    return (sb(f"{tag}_lg", [P, TT, E]), sb(f"{tag}_mx", [P, TT]), sb(f"{tag}_ez", [P, TT, E]),
            sb(f"{tag}_rs", [P, TT]), sb(f"{tag}_top", [P, TT, 8]), sb(f"{tag}_ix", [P, TT, 8], U32),
            sb(f"{tag}_ixf", [P, TT, 8]), sb(f"{tag}_oh", [P, 2, TT, E]))


class Space:

    def __init__(self, nc, ctx, tag):
        self.nc, self.ctx, self.tag, self.sems = nc, ctx, tag, []
        ctx.callback(self.clear)

    def sb(self, name, shape, dt=F32):
        return self.ctx.enter_context(self.nc.sbuf_tensor(f"{self.tag}_{name}", shape, dt))

    def sem(self, name):
        self.sems.append(self.nc.alloc_semaphore(name=f"{self.tag}_{name}"))
        return self.sems[-1]

    def clear(self):
        self.nc.clear_and_free_semaphores(self.sems)
        self.nc.all_engine_barrier()


def phase_ffn0(nc, io, X, bank, ident, iota, apart):
    E, H = 8, 256
    with ExitStack() as ctx:
        sp = Space(nc, ctx, "f0")
        sb, sem = sp.sb, sp.sem
        w_in = [sb("w_shared_in", [P, KD, 2 * H]), sb("w1_shared", [P, KD, 2 * H])]
        w_out = sb("w_shared_out", [P, KD, D])
        w2 = sb("w2", [P, KD, E * D])
        wg = sb("w_gate", [P, KD, E])
        gb = sb("gate_bias", [P, E])
        work = ln_work(sb, "ln")
        xn = sb("xn", [P, TT, D])
        xT = sb("xT", [P, KD, S])
        gate = sb("silu", [P, 2, 2 * S])
        hT = sb("hT", [P, 2, 2 * S])
        rw = route_work(sb, "route", E)
        lg, ez, oh = rw[0], rw[2], rw[7]
        weights = sem("weights")
        xn_ready, xt_turned, xt_ready = sem("xn_ready"), sem("xt_turned"), sem("xt_ready")
        logits_done, z_ready, exp_ready = sem("logits_done"), sem("z_ready"), sem("exp_ready")
        up_done, silu_ready, hidden_ready = sem("up_done"), sem("silu_ready"), sem("hidden_ready")
        shared_done, part_done, part_used = sem("shared_done"), sem("part_done"), sem("part_used")
        own, sem_first = sem("vector_steps"), sem("first_steps")
        RING = [bank[4], bank[5], bank[7]]
        PARTS = TT * E // 2
        TURN = ROUTE_STEPS + 2 + LN_STEPS + TT + PARTS
        lg_ps = bank[1][:, 0:TT * E].rearrange("p (t e) -> p t e", t=TT)
        block = ctx.enter_context(nc.Block())

        @block.sync
        def _(sp_):
            sp_.dma_start(wg[:, :, :], io["L0_ffn_w_gate"].rearrange("(k p) e -> p k e", p=P)).then_inc(weights, 16)
            sp_.dma_start(gb[:, :], io["L0_ffn_gate_bias"].rearrange("(a e) -> a e", a=1).to_broadcast([P, E])).then_inc(weights, 16)
            sp_.dma_start(w_in[0][:, :, :], io["L0_ffn_w_shared_in"].rearrange("(k p) n -> p k n", p=P)).then_inc(weights, 16)
            sp_.dma_start(w_in[1][:, :, :], io["L0_ffn_w1_shared"].rearrange("(k p) n -> p k n", p=P)).then_inc(weights, 16)
            sp_.dma_start(w_out[:, :, :], io["L0_ffn_w_shared_out"].rearrange("(k p) n -> p k n", p=P)).then_inc(weights, 16)
            for k in range(KD):
                sp_.dma_start(w2[:, k, :].rearrange("p (e n) -> p e n", e=E),
                              io["L0_ffn_w2"][:, k * P:(k + 1) * P, :].rearrange("e p n -> p e n")).then_inc(weights, 16)

        @block.tensor
        def _(pe):
            def turn_x(b):
                pe.wait_ge(xn_ready, b + 1)
                turn_tokens(pe, bank[0], xn, ident).then_inc(xt_turned, 1)

            def turn(b, last):
                pe.wait_ge(xt_ready, b + 1)
                for t in range(TT):
                    for k in range(KD):
                        mm = pe.matmul(lg_ps[:, t, :], xT[:, k, t * P:(t + 1) * P], wg[:, k, :],
                                       start=(k == 0), stop=(k == KD - 1))
                mm.then_inc(logits_done, 1)
                for which in range(2):
                    if which == 1:
                        pe.wait_ge(part_used, b * PARTS + 1)
                    for n in range(4):
                        ps = bank[2 + 2 * which + n // 2]
                        for k in range(KD):
                            mm = pe.matmul(ps[:, (n % 2) * S:(n % 2) * S + S],
                                           w_in[which][:, k, n * P:(n + 1) * P], xT[:, k, :],
                                           start=(k == 0), stop=(k == KD - 1))
                    mm.then_inc(up_done, 1)
                if not last:
                    turn_x(b + 1)
                pe.wait_ge(hidden_ready, b * 2 + 1)
                for t in range(TT):
                    for k in range(KD):
                        mm = pe.matmul(bank[6][:, t * D:(t + 1) * D], hT[:, 0, k * S + t * P:k * S + t * P + P],
                                       w_out[:, k, :], start=(k == 0), stop=(k == KD - 1))
                mm.then_inc(shared_done, 1)
                pe.wait_ge(hidden_ready, b * 2 + 2)
                for g in range(PARTS):
                    t, pair = g // (E // 2), g % (E // 2)
                    if g >= 3:
                        pe.wait_ge(part_used, b * PARTS + g - 1)
                    for k in range(KD):
                        mm = pe.matmul(RING[g % 3][:, :], hT[:, 1, k * S + t * P:k * S + t * P + P],
                                       w2[:, k, pair * 2 * D:(pair + 1) * 2 * D], start=(k == 0), stop=(k == KD - 1))
                    mm.then_inc(part_done, 1)

            pe.wait_ge(weights, 16 * 7)
            turn_x(0)
            with pe.Fori(0, B - 1) as b:
                turn(b, False)
            turn(B - 1, True)

        @block.scalar
        def _(act):
            with act.Fori(0, B) as b:
                act.wait_ge(xt_turned, b + 1)
                act.activation(xT[:, :, :].rearrange("p k s -> p (k s)"), bank[0][:, :], ACT.Copy).then_inc(xt_ready, 1)
                act.wait_ge(z_ready, b + 1)
                act.activation(ez[:, :, :], lg[:, :, :], ACT.Exp).then_inc(exp_ready, 1)
                for which in range(2):
                    act.wait_ge(up_done, b * 2 + which + 1)
                    act.activation(gate[:, which, :], bank[2 + 2 * which][:, :], ACT.Silu).then_inc(silu_ready, 1)

        @block.vector
        def _(dve):
            def turn(b, last):
                st = Steps(dve, own, b * TURN, TURN - LN_STEPS * last)
                dve.wait_ge(logits_done, b + 1)
                route(dve, st, E, lg_ps, bc(gb[:, None, :], [P, TT, E]), rw, iota, z_ready, exp_ready, b, apart)
                st.step(dve.tensor_tensor(oh[:, 0, :, :], oh[:, 0, :, :], oh[:, 1, :, :], ALU.add))
                st.step(dve.tensor_tensor(lg[:, :, :], ez[:, :, :], oh[:, 0, :, :], ALU.mult))
                for which in range(2):
                    dve.wait_ge(silu_ready, b * 2 + which + 1)
                    dve.tensor_tensor(hT[:, which, :], gate[:, which, :], bank[3 + 2 * which][:, :],
                                      ALU.mult).then_inc(hidden_ready, 1)
                if not last:
                    layer_norm(dve, st, X, b * TT + TT, work, xn, xn_ready, apart)
                dve.wait_ge(shared_done, b + 1)
                for t in range(TT):
                    st.step(dve.tensor_tensor(X[:, b * TT + t, :], bank[6][:, t * D:(t + 1) * D],
                                              X[:, b * TT + t, :], ALU.add))
                for g in range(PARTS):
                    t, pair = g // (E // 2), g % (E // 2)
                    dve.wait_ge(part_done, b * PARTS + g + 1)
                    for e in range(2):
                        i = dve.scalar_tensor_tensor(X[:, b * TT + t, :], RING[g % 3][:, e * D:(e + 1) * D],
                                                     lg[:, t, 2 * pair + e:2 * pair + e + 1],
                                                     X[:, b * TT + t, :], ALU.mult, ALU.add)
                        if e == 0:
                            st.step(i)
                        else:
                            i.then_inc(part_used, 1)
                            dve.wait_ge(part_used, b * PARTS + g + 2)
                st.end()

            dve.sem_inc(part_used, 1)
            first = Steps(dve, sem_first, 0, LN_STEPS)
            layer_norm(dve, first, X, 0, work, xn, xn_ready, apart)
            dve.wait_ge(weights, 16 * 7)
            with dve.Fori(0, B - 1) as b:
                turn(b, False)
            turn(B - 1, True)



HEADS, HD = 16, 16
TERMS = 6
ROWS = TERMS * HD
AUG = 3
Q_PART = (0, 0, 0, 1, 1, 2)
K_PART = (0, 1, 2, 0, 1, 0)
GROUPS = HEADS // 2


def phase_attention(nc, io, X, C, CT, PS, ident, iota, apart, layer):
    shared_kv = layer == 1
    KH = 1 if shared_kv else HEADS
    PIECES = {1: ["xT", None, "qp", "kvp", "sc", None, "ohT", "mkv"],
              2: ["xT", None, "qp", "kp", None, None, None, None],
              3: ["xT", None, "qp", "kp", "v", None, None, None]}[layer]
    PROJ = [("pr", (0, 1))] if layer == 2 else [("pr0", (0,)), ("pr1", (1,))]
    TAIL = ["oT"] + [name for name, _ in PROJ]

    def uses(has_a, has_f):
        out = []
        for g in range(GROUPS):
            if has_a and g < 6:
                out += [("A", i) for i in range(16 * g // 6, 16 * (g + 1) // 6)]
            if has_f and PIECES[g]:
                out.append(PIECES[g])
            if has_a and g == 7:
                out.append("nm")
        return out

    FRONT = [p for p in PIECES if p]
    PRO = [FRONT, FRONT, [("A", i) for i in range(16)] + ["nm"]]
    START = sum(len(p) for p in PRO)
    FULL = uses(True, True) + TAIL
    assert len(FULL) % 2 == 0

    class Ring:

        def __init__(self, names, fixed, b):
            self.names, self.fixed, self.b = names, fixed, b

        def bank(self, name):
            return 4 + (self.fixed + self.names.index(name)) % 2

        def filled(self, name):
            return self.b * len(FULL) + self.fixed + self.names.index(name) + 1

        def taken(self, name):
            return self.emptied_before(name) + 1

        def emptied_before(self, name):
            return self.b * (len(FULL) // 2) + (self.fixed + self.names.index(name)) // 2

        def first_on_bank(self, name):
            return isinstance(self.b, int) and self.emptied_before(name) == 0

    apart, apart_pool, apart_sync, apart_pe = apart
    with ExitStack() as ctx:
        sp = Space(nc, ctx, f"a{layer}")
        sb, sem = sp.sb, sp.sem
        wq = sb("w_q", [P, KD, D])
        wo = sb("w_o", [P, KD, D])
        wk = sb("w_k", [P, KD, 2 * HD if shared_kv else D])
        wv = sb("w_v", [P, KD, D]) if layer == 3 else None
        if layer > 1:
            bq, bk = sb("b_q", [P, KD]), sb("b_k", [P, KD])
            bo = sb("b_o", [P, D])
        bv = sb("b_v", [P, D]) if layer == 3 else None
        work = ln_work(sb, "ln")
        xn = sb("xn", [P, TT, D])
        xT, oT = sb("xT", [P, KD, S]), sb("oT", [P, KD, S])
        cT = sb("cT", [P, KD, S]) if layer != 2 else None
        qT = sb("qT", [P, KD, S])
        kT = sb("kT", [P, KD, S]) if not shared_kv else sb("kT", [HD, 1, S])
        KP = kT.shape[0]
        q_rest, k_rest = sb("q_rest", [P, KD, S]), sb("k_rest", list(kT.shape))
        q_parts = sb("q_parts", [P, 3, KD, S], BF16)
        k_parts = sb("k_parts", [KP, 3, kT.shape[1], S], BF16)
        Q = [sb(f"q_stack{i}", [ROWS + AUG, HEADS, S], BF16) for i in range(2)]
        K = [sb(f"k_stack{i}", [ROWS + AUG, KH, S], BF16) for i in range(2)]
        probs = sb("probs", [P, 2, 2, 2, S])
        MX = sb("row_max", [P, TT, HEADS])
        nm, nm_rest = sb("neg_max", [HEADS, S]), sb("neg_max_rest", [HEADS, S])
        nm_parts = sb("neg_max_parts", [HEADS, AUG, S], BF16)
        rec = sb("reciprocal", [P, TT, HEADS])
        att = sb("att", [P, TT, D])
        V = sb("v", [P, B * TT, KH, HD + 1])
        if shared_kv:
            kvp = sb("kv_proj", [P, TT, 2 * HD])
            top, ix, ixf = sb("top", [P, TT, 8]), sb("ix", [P, TT, 8], U32), sb("ixf", [P, TT])
            oh, ohT = sb("one_hot", [P, TT, S]), sb("one_hotT", [P, TT, S])
            oh_ready = sem("one_hot_ready")
        weights, const_ready = sem("weights"), sem("constants_ready")
        xn_ready, cT_ready = sem("xn_ready"), sem("cT_ready")
        q_split, k_split = sem("q_split"), sem("k_split")
        stacked = [sem("stacked0"), sem("stacked1")]
        nm_split, nm_stacked = sem("nm_split"), sem("nm_stacked")
        ring_filled = sem("ring_filled")
        ring_emptied = [sem("bank4_emptied"), sem("bank5_emptied")]
        logits_done, exp_done, pv_done = sem("logits_done"), sem("exp_done"), sem("pv_done")
        att_ready, x_added = sem("att_ready"), sem("x_added")
        bias_ready = sem("bias_ready")
        parts_out = sem("parts_out")
        own_v, own_p = sem("vector_steps"), sem("pool_steps")
        block = ctx.enter_context(nc.Block())
        n_weights = {1: 3, 2: 6, 3: 8}[layer]
        FILL = 16 * 2 * TERMS
        q_dram = nc.dram_tensor(f"a{layer}_q_parts_dram", [2, 3, D, S], BF16, kind="Internal").ap()
        k_dram = nc.dram_tensor(f"a{layer}_k_parts_dram", [2, 3, KH * HD, S], BF16, kind="Internal").ap()

        def run(turn, prologue, eng):
            prologue()
            with eng.Fori(0, (B - 2) // 2) as pair:
                for par in range(2):
                    turn((2 * pair + par, par, pair + 1), (2 * pair + par + 1, 1 - par, pair + par + 1),
                         (2 * pair + par + 2, par, pair + 2), Ring(FULL, START + par * len(FULL), 2 * pair))
            at = START + (B - 2) * len(FULL)
            for b in (B - 2, B - 1):
                names = uses(b + 1 < B, False) + TAIL
                turn((b, b % 2, b // 2 + 1), (b + 1, (b + 1) % 2, (b + 1) // 2 + 1) if b + 1 < B else None,
                     None, Ring(names, at, 0))
                at += len(names)

        def start_rings():
            at, out = 0, []
            for names in PRO:
                out.append(Ring(names, at, 0))
                at += len(names)
            return out

        @block.sync
        def _(sync):
            def kxm(name):
                return io[name].rearrange("(k p) n -> p k n", p=P)

            if layer == 1:
                sync.dma_start(wq[:, :, :], kxm("L1_xattn_WqT")).then_inc(weights, 16)
                sync.dma_start(wk[:, :, :], kxm("L1_xattn_WkvT")).then_inc(weights, 16)
                sync.dma_start(wo[:, :, :], kxm("L1_xattn_WcT")).then_inc(weights, 16)
            elif layer == 2:
                sync.dma_start(wq[:, :, :], kxm("L2_xattn_WqT")).then_inc(weights, 16)
                sync.dma_start(wk[:, :, :], kxm("L2_xattn_WkT")).then_inc(weights, 16)
                sync.dma_start(wo[:, :, :], kxm("L2_xattn_WcT")).then_inc(weights, 16)
                bias_names = ("L2_xattn_bq", "L2_xattn_bk", "L2_xattn_bc")
            else:
                sync.dma_start(wq[:, :, :], kxm("L3_xattn_w_q")).then_inc(weights, 16)
                wkv = io["L3_xattn_w_kv"].rearrange("(k p) (a n) -> p k a n", p=P, a=2)
                sync.dma_start(wk[:, :, :], wkv[:, :, 0, :]).then_inc(weights, 16)
                sync.dma_start(wv[:, :, :], wkv[:, :, 1, :]).then_inc(weights, 16)
                sync.dma_start(wo[:, :, :], kxm("L3_xattn_w_out")).then_inc(weights, 16)
                sync.dma_start(bv[:, :], io["L3_xattn_b_kv"][D:2 * D].rearrange("(a n) -> a n", a=1)
                               .to_broadcast([P, D])).then_inc(weights, 16)
                bias_names = ("L3_xattn_b_q", "L3_xattn_b_kv", "L3_xattn_b_out")
            if layer > 1:
                for tile, name in ((bq, bias_names[0]), (bk, bias_names[1])):
                    sync.dma_start(tile[:, :], io[name][0:D].rearrange("(k p) -> p k", p=P),
                                   allow_slow_non_contiguous=True).then_inc(weights, 16)
                sync.dma_start(bo[:, :], io[bias_names[2]].rearrange("(a n) -> a n", a=1)
                               .to_broadcast([P, D])).then_inc(weights, 16)

            def stack(f, before):
                b, par, fill = f
                if before is not None:
                    wait_apart(sync, logits_done, GROUPS * before + GROUPS, apart_sync)
                sync.wait_ge(q_split, b + 1)
                sync.dma_start(q_dram[par].rearrange("s (k p) l -> p s k l", p=P), q_parts[:, :, :, :]).then_inc(parts_out, 16)
                sync.wait_ge(k_split, b + 1)
                if shared_kv:
                    sync.dma_start(k_dram[par].rearrange("s p l -> p s l"), k_parts[:, :, 0, :]).then_inc(parts_out, 16)
                else:
                    sync.dma_start(k_dram[par].rearrange("s (k p) l -> p s k l", p=P), k_parts[:, :, :, :]).then_inc(parts_out, 16)
                wait_apart(sync, parts_out, 32 * b + 32, apart_sync)
                for stacks, dram, order in ((Q, q_dram, Q_PART), (K, k_dram, K_PART)):
                    for c in range(TERMS):
                        sync.dma_start(stacks[par][c * HD:(c + 1) * HD, :, :],
                                       dram[par, order[c]].rearrange("(h d) l -> d h l", d=HD)).then_inc(stacked[par], 16)

            def stack_max(a):
                b, par, fill = a
                sync.wait_ge(nm_split, b + 1)
                for s in range(AUG):
                    sync.dma_start(Q[par][ROWS + s:ROWS + s + 1, :, :], nm_parts[:, s:s + 1, :]).then_inc(nm_stacked, 16)

            def prologue():
                stack((0, 0, 1), None)
                stack((1, 1, 1), None)
                stack_max((0, 0, 1))

            def turn(now, a, f, ring):
                if f:
                    stack(f, now[0])
                if a:
                    stack_max(a)
            run(turn, prologue, sync)

        @block.gpsimd
        def _(pool):
            for n, ones in enumerate((K[0][ROWS:ROWS + AUG, :, :], K[1][ROWS:ROWS + AUG, :, :], V[:, :, :, HD:HD + 1])):
                pool.memset(ones, 1.0).then_inc(const_ready, 1)
                pool.wait_ge(const_ready, n + 1)
            if layer == 2:
                pool.tensor_copy(V[:, :, :, 0:HD], C[:, :, :].rearrange("p t (h d) -> p t h d", d=HD)).then_inc(const_ready, 1)
                pool.wait_ge(const_ready, 4)

            def split(st, src, rest, parts, done):
                st.step(pool.tensor_copy(parts(0), src))
                st.step(pool.tensor_tensor(rest, src, parts(0), ALU.subtract), apart_pool)
                st.step(pool.tensor_copy(parts(1), rest))
                st.step(pool.tensor_tensor(rest, rest, parts(1), ALU.subtract), apart_pool)
                pool.tensor_copy(parts(2), rest).then_inc(done, 1)

            def split_qk(st, ring, f, fill_before):
                b, par, fill = f
                k_name = "mkv" if shared_kv else "kp"
                if fill_before is not None:
                    wait_apart(pool, parts_out, 32 * b, apart_pool)
                wait_apart(pool, ring_emptied[ring.bank("qp") - 4], ring.taken("qp"), apart_pool)
                split(st, qT[:, :, :], q_rest[:, :, :], lambda s: q_parts[:, s, :, :], q_split)
                wait_apart(pool, ring_emptied[ring.bank(k_name) - 4], ring.taken(k_name), apart_pool)
                split(st, kT[:, :, :], k_rest[:, :, :], lambda s: k_parts[:, s, :, :], k_split)

            def split_max(st, ring, a):
                b, par, fill = a
                wait_apart(pool, ring_emptied[ring.bank("nm") - 4], ring.taken("nm"), apart_pool)
                if not (isinstance(b, int) and b == 0):
                    wait_apart(pool, nm_stacked, 16 * AUG * b, apart_pool)
                split(st, nm[:, :], nm_rest[:, :], lambda s: nm_parts[:, s, :], nm_split)

            def prologue():
                st = Steps(pool, own_p, 0, 20)
                r = start_rings()
                split_qk(st, r[0], (0, 0, 1), None)
                split_qk(st, r[1], (1, 1, 1), 1)
                split_max(st, r[2], (0, 0, 1))
                st.end()

            def turn(now, a, f, ring):
                before = 20 + now[0] * 12 if a else 20 + (B - 2) * 12 + 4
                st = Steps(pool, own_p, before, 4 * (2 * bool(f) + bool(a)))
                if f:
                    split_qk(st, ring, f, f[2] - (1 if f[1] == 0 else 0))
                if a:
                    split_max(st, ring, a)
                st.end()
            run(turn, prologue, pool)

        @block.tensor
        def _(pe):
            def fill(ring, name):
                if not ring.first_on_bank(name):
                    pe.wait_ge(ring_emptied[ring.bank(name) - 4], ring.emptied_before(name))
                return PS[:, ring.bank(name), :]

            def copied(ring, name):
                pe.wait_ge(ring_emptied[ring.bank(name) - 4], ring.taken(name))

            def project(out, w, src, n_out):
                for n in range(n_out):
                    for k in range(KD):
                        mm = pe.matmul(out[:, n * S:(n + 1) * S], w[:, k, n * P:(n + 1) * P], src[:, k, :],
                                       start=(k == 0), stop=(k == KD - 1))
                return mm

            def front(ring, name, f):
                b, par, _ = f
                if name == "xT":
                    pe.wait_ge(xn_ready, b + 1)
                    mm = turn_tokens(pe, fill(ring, name), xn, ident)
                if name == "qp":
                    copied(ring, "xT")
                    mm = project(fill(ring, name), wq, xT, KD)
                if name == "kp":
                    mm = project(fill(ring, name), wk, CT[:, :, bass.ds(b * S, S)], KD)
                if name == "v":
                    pe.wait_ge(cT_ready, b + 1)
                    ps = fill(ring, name)
                    for t in range(TT):
                        for k in range(KD):
                            mm = pe.matmul(ps[:, t * D:(t + 1) * D], cT[:, k, t * P:(t + 1) * P], wv[:, k, :],
                                           start=(k == 0), stop=(k == KD - 1))
                if name == "kvp":
                    pe.wait_ge(cT_ready, b + 1)
                    ps = fill(ring, name)
                    for t in range(TT):
                        for k in range(KD):
                            mm = pe.matmul(ps[:, t * 2 * HD:(t + 1) * 2 * HD], cT[:, k, t * P:(t + 1) * P], wk[:, k, :],
                                           start=(k == 0), stop=(k == KD - 1))
                if name == "sc":
                    copied(ring, "qp")
                    ps = fill(ring, name)
                    for t in range(TT):
                        for k in range(KD):
                            mm = pe.matmul(ps[:, t * S:(t + 1) * S], qT[:, k, t * P:(t + 1) * P], cT[:, k, :],
                                           start=(k == 0), stop=(k == KD - 1))
                if name == "ohT":
                    pe.wait_ge(oh_ready, b + 1)
                    mm = turn_tokens(pe, fill(ring, name), oh, ident)
                if name == "mkv":
                    copied(ring, "kvp")
                    copied(ring, "ohT")
                    ps = fill(ring, name)
                    for t in range(TT):
                        pe.matmul(ps[0:HD, 0:S], kvp[:, t, 0:HD], ohT[:, t, :], start=(t == 0), stop=(t == TT - 1))
                    for t in range(TT):
                        for m in range(TT):
                            mm = pe.matmul(ps[:, S + t * HD:S + (t + 1) * HD], ohT[:, m, t * P:(t + 1) * P],
                                           kvp[:, m, HD:2 * HD], start=(m == 0), stop=(m == TT - 1))
                mm.then_inc(ring_filled, 1)

            def piece_a(ring, i, a):
                b, par, fill_no = a
                if i == 0:
                    pe.wait_ge(stacked[par], FILL * fill_no)
                t, h = i // GROUPS, 2 * (i % GROUPS)
                ps = fill(ring, ("A", i))
                for j in range(2):
                    mm = pe.matmul(ps[:, j * S:(j + 1) * S], Q[par][0:ROWS, h + j, t * P:(t + 1) * P],
                                   K[par][0:ROWS, 0 if shared_kv else h + j, :], start=True, stop=True)
                mm.then_inc(ring_filled, 1)

            def turn_max(ring, a):
                for i in (14, 15):
                    copied(ring, ("A", i))
                ps = fill(ring, "nm")
                for t in range(TT):
                    mm = pe.transpose(ps[0:HEADS, t * P:(t + 1) * P], MX[:, t, :], ident[:, :])
                mm.then_inc(ring_filled, 1)

            def logits(now, g):
                b, par, _ = now
                if g == 0:
                    pe.wait_ge(nm_stacked, 16 * AUG * b + 16 * AUG)
                for m in range(TT):
                    for j in range(2):
                        h = 2 * g + j
                        mm = pe.matmul(PS[:, 2 * (g % 2) + m, j * S:(j + 1) * S],
                                       K[par][:, 0 if shared_kv else h, m * P:(m + 1) * P], Q[par][:, h, :],
                                       start=True, stop=True)
                mm.then_inc(logits_done, 1)

            def pv(now, g):
                b, par, _ = now
                if g == 0:
                    pe.wait_ge(att_ready, b)
                pe.wait_ge(exp_done, b * GROUPS + g + 1)
                for j in range(2):
                    h = 2 * g + j
                    for t in range(TT):
                        for m in range(TT):
                            v = V[:, b * TT + m, 0 if shared_kv else h, :]
                            mm = pe.matmul(PS[:, 6 + t, h * (HD + 1):(h + 1) * (HD + 1)],
                                           probs[:, g % 2, m, j, t * P:(t + 1) * P], v, start=(m == 0), stop=(m == TT - 1))
                mm.then_inc(pv_done, 1)

            def prologue():
                pe.wait_ge(weights, 16 * n_weights)
                pe.wait_ge(const_ready, 4 if layer == 2 else 3)
                r = start_rings()
                for i in range(2):
                    for name in FRONT:
                        front(r[i], name, (i, i, 1))
                for i in range(16):
                    piece_a(r[2], i, (0, 0, 1))
                turn_max(r[2], (0, 0, 1))

            def turn(now, a, f, ring):
                b = now[0]
                for g in range(GROUPS):
                    logits(now, g)
                    if a and g < 6:
                        for i in range(16 * g // 6, 16 * (g + 1) // 6):
                            piece_a(ring, i, a)
                    if g:
                        pv(now, g - 1)
                    if f and PIECES[g]:
                        front(ring, PIECES[g], f)
                    if a and g == 7:
                        turn_max(ring, a)
                pv(now, GROUPS - 1)
                pe.wait_ge(att_ready, b + 1)
                turn_tokens(pe, fill(ring, "oT"), att, ident).then_inc(ring_filled, 1)
                copied(ring, "oT")
                for name, tiles in PROJ:
                    ps = fill(ring, name)
                    for t in tiles:
                        for k in range(KD):
                            mm = pe.matmul(ps[:, t * D:(t + 1) * D], oT[:, k, t * P:(t + 1) * P], wo[:, k, :],
                                           start=(k == 0), stop=(k == KD - 1))
                    mm.then_inc(ring_filled, 1)
            run(turn, prologue, pe)

        @block.scalar
        def _(act):
            def take(ring, name, dst, waits=None, **how):
                act.wait_ge(ring_filled, ring.filled(name))
                act.activation(dst, PS[0:dst.shape[0], ring.bank(name), 0:512 if dst.shape[0] == P else S], ACT.Copy, **how
                               ).then_inc(ring_emptied[ring.bank(name) - 4], 1)

            def flat(tile):
                return tile[:, :, :].rearrange("p k s -> p (k s)")

            def take_biased(ring, name, dst, bias, scale):
                act.wait_ge(ring_filled, ring.filled(name))
                for k in range(KD):
                    i = act.activation(dst[:, k, :], PS[:, ring.bank(name), k * S:(k + 1) * S], ACT.Identity,
                                       bias=bias[:, k:k + 1], scale=scale)
                i.then_inc(ring_emptied[ring.bank(name) - 4], 1)

            def front(ring, name, f):
                b = f[0]
                later = not isinstance(b, int) or b > 0
                if name == "xT":
                    take(ring, name, flat(xT))
                    if layer != 2:
                        act.activation(cT[:, :, :], CT[:, :, bass.ds(b * S, S)], ACT.Copy).then_inc(cT_ready, 1)
                if name == "qp":
                    if later:
                        act.wait_ge(q_split, b)
                    if layer == 1:
                        take(ring, name, flat(qT), scale=HD ** -0.5)
                    else:
                        take_biased(ring, name, qT, bq, HD ** -0.5)
                if name == "kp":
                    if later:
                        act.wait_ge(k_split, b)
                    take_biased(ring, name, kT, bk, 1.0)
                if name == "ohT":
                    take(ring, name, flat(ohT))

            def take_max(ring, a):
                b = a[0]
                if not (isinstance(b, int) and b == 0):
                    act.wait_ge(nm_split, b)
                take(ring, "nm", nm[:, :], scale=-1.0)

            def exp(now, g):
                b = now[0]
                act.wait_ge(logits_done, b * GROUPS + g + 1)
                act.wait_ge(pv_done, b * GROUPS + max(g - 1, 0))
                act.activation(probs[:, g % 2, :, :, :].rearrange("p m h s -> p (m h s)"),
                               PS[:, 2 * (g % 2):2 * (g % 2) + 2, :].rearrange("p m n -> p (m n)"), ACT.Exp
                               ).then_inc(exp_done, 1)

            def prologue():
                if layer > 1:
                    act.wait_ge(weights, 16 * n_weights)
                    act.activation(bq[:, :], bq[:, :], ACT.Copy, scale=HD ** -0.5).then_inc(bias_ready, 1)
                    act.wait_ge(bias_ready, 1)
                r = start_rings()
                for i in range(2):
                    for name in FRONT:
                        front(r[i], name, (i, i, 1))
                take_max(r[2], (0, 0, 1))

            def turn(now, a, f, ring):
                for g in range(GROUPS):
                    exp(now, g)
                    if f and PIECES[g]:
                        front(ring, PIECES[g], f)
                    if a and g == 7:
                        take_max(ring, a)
                act.wait_ge(ring_filled, ring.filled("oT"))
                take(ring, "oT", flat(oT))
            run(turn, prologue, act)

        @block.vector
        def _(dve):
            def emptied(ring, name):
                return ring_emptied[ring.bank(name) - 4]

            def front(st, ring, name, f):
                b = f[0]
                ps = PS[:, ring.bank(name), :]
                if name == "kvp":
                    dve.wait_ge(ring_filled, ring.filled(name))
                    dve.tensor_copy(kvp[:, :, :].rearrange("p t n -> p (t n)"), ps[:, 0:TT * 2 * HD]).then_inc(emptied(ring, name), 1)
                if name == "sc":
                    dve.wait_ge(ring_filled, ring.filled(name))
                    dve.sem_inc(apart, 1)
                    for t in range(TT):
                        st.step(dve.max(top[:, t, :], ps[:, t * S:(t + 1) * S]), apart)
                    for t in range(TT):
                        i = dve.max_index(ix[:, t, :], top[:, t, :], ps[:, t * S:(t + 1) * S])
                        if t == 0:
                            st.step(i, apart)
                    i.then_inc(emptied(ring, name), 1)
                    dve.wait_ge(emptied(ring, name), ring.taken(name))
                    st.step(dve.tensor_copy(ixf[:, :], ix[:, :, 0]))
                    for t in range(TT):
                        i = dve.tensor_scalar(oh[:, t, :], iota[:, 0:S], ixf[:, t:t + 1], None, ALU.is_equal)
                    i.then_inc(oh_ready, 1)
                if name == "mkv":
                    later = not isinstance(b, int) or b > 0
                    dve.wait_ge(ring_filled, ring.filled(name))
                    if later:
                        dve.wait_ge(k_split, b)
                    st.step(dve.tensor_copy(kT[:, 0, :], ps[0:HD, 0:S]))
                    dve.tensor_copy(V[:, bass.ds(b * TT, TT), 0, 0:HD], ps[:, S:S + TT * HD].rearrange("p (t d) -> p t d", t=TT)
                                    ).then_inc(emptied(ring, name), 1)
                if name == "v":
                    dve.wait_ge(ring_filled, ring.filled(name))
                    for t in range(TT):
                        i = dve.tensor_tensor(V[:, b * TT + t, :, 0:HD], ps[:, t * D:(t + 1) * D].rearrange("p (h d) -> p h d", h=HEADS),
                                              bv[:, :].rearrange("p (h d) -> p h d", h=HEADS), ALU.add)
                    i.then_inc(emptied(ring, name), 1)

            FRONT_STEPS = {1: 2 + 1 + 1 + 1, 2: 0, 3: 0}[layer]

            def row_max(ring, i):
                t, h = i // GROUPS, 2 * (i % GROUPS)
                name = ("A", i)
                dve.wait_ge(ring_filled, ring.filled(name))
                dve.tensor_reduce(MX[:, t, h:h + 2], PS[:, ring.bank(name), :].rearrange("p (h m) -> p h m", h=2),
                                  AX.X, ALU.max).then_inc(emptied(ring, name), 1)

            def prologue():
                st = Steps(dve, own_v, 0, 2 * (LN_STEPS + FRONT_STEPS))
                r = start_rings()
                dve.wait_ge(weights, 16 * n_weights)
                for i in range(2):
                    if i:
                        dve.wait_ge(ring_filled, r[0].filled("xT"))
                    layer_norm(dve, st, X, i * TT, work, xn, xn_ready, apart)
                    for name in FRONT:
                        front(st, r[i], name, (i, i, 1))
                for i in range(16):
                    row_max(r[2], i)
                st.end()

            START_STEPS = 2 * (LN_STEPS + FRONT_STEPS)
            BACK_STEPS = 1 + (TT if layer > 1 else 0)

            def turn(now, a, f, ring):
                b = now[0]
                before = START_STEPS + b * (LN_STEPS + FRONT_STEPS + BACK_STEPS)
                if not a:
                    before -= LN_STEPS + FRONT_STEPS
                st = Steps(dve, own_v, before,
                           BACK_STEPS + (LN_STEPS + FRONT_STEPS) * bool(f))
                if f:
                    layer_norm(dve, st, X, f[0] * TT, work, xn, xn_ready, apart)
                for g in range(GROUPS):
                    if a and g < 6:
                        for i in range(16 * g // 6, 16 * (g + 1) // 6):
                            row_max(ring, i)
                    if f and PIECES[g]:
                        front(st, ring, PIECES[g], f)
                dve.wait_ge(pv_done, GROUPS * b + GROUPS)
                out = PS[:, 6:8, 0:HEADS * (HD + 1)].rearrange("p t (h d) -> p t h d", d=HD + 1)
                st.step(dve.reciprocal(rec[:, :, :], out[:, :, :, HD]))
                dve.tensor_tensor(att[:, :, :].rearrange("p t (h d) -> p t h d", d=HD), out[:, :, :, 0:HD],
                                  bc(rec[:, :, :, None], [P, TT, HEADS, HD]), ALU.mult).then_inc(att_ready, 1)
                if layer > 1:
                    for t in range(TT):
                        st.step(dve.tensor_tensor(X[:, b * TT + t, :], X[:, b * TT + t, :], bo[:, :], ALU.add))
                for name, tiles in PROJ:
                    dve.wait_ge(ring_filled, ring.filled(name))
                    for t in tiles:
                        i = dve.tensor_tensor(X[:, b * TT + t, :], PS[:, ring.bank(name), t * D:(t + 1) * D],
                                              X[:, b * TT + t, :], ALU.add)
                    i.then_inc(emptied(ring, name), 1)
                st.end()
            run(turn, prologue, dve)


def in_pairs(eng, turn):
    with eng.Fori(0, B // 2 - 1) as pair:
        for par in range(2):
            turn(2 * pair + par, par, False)
    turn(B - 2, 0, False)
    turn(B - 1, 1, True)


def phase_ffn2(nc, io, X, PS, ident, iota, apart, later_than, all_ones):
    E, H, CAP, TOP = 16, 128, 2 * S // 16, 2
    SLOTS = E * CAP
    EG, NG = P // CAP, E * CAP // P
    apart_v, apart_pool, apart_sync, apart_pe = apart
    with ExitStack() as ctx:
        sp = Space(nc, ctx, "f2")
        sb, sem = sp.sb, sp.sem
        wr = sb("w_router", [P, KD, E])
        w_up = sb("w_up", [P, 2, EG, 2, KD, H])
        w_pr = sb("w_proj", [P, 2, EG, D])
        work = ln_work(sb, "ln")
        xn = [sb(f"xn{i}", [P, TT, D]) for i in range(2)]
        xT = sb("xT", [P, KD, S])
        rw = route_work(sb, "route", E)
        lg, ez, ixf, oh = rw[0], rw[2], rw[6], rw[7]
        tmp = sb("tmp", [P, TOP, TT, E])
        prob, place, slot, got = (sb(n, [P, TOP, TT]) for n in ("prob", "place", "slot", "slot_collected"))
        Dm, Wm, W2 = sb("dispatch", [P, TT, SLOTS]), sb("collect", [P, TT, SLOTS]), sb("collect2", [P, TT, SLOTS])
        xd = sb("x_dispatched", [P, KD, E, B, CAP])
        WT = sb("collectT", [P, B, NG, S])
        gate, hid = sb("silu", [P, 2, B * CAP]), sb("hidden", [P, 2, B * CAP])
        out = sb("expert_out", [P, NG, B, D])
        names = ("weights", "xn_ready", "xT_turned", "xT_ready", "logits_done", "z_ready", "exp_ready", "choice_ready",
                 "place_done", "dispatch_ready", "dispatched", "dispatched_copied", "slots_ready", "collect_ready",
                 "collect_turned0", "collect_turned1", "collect_copied",
                 "up_done", "silu_ready", "hidden_ready", "down_done", "out_copied", "y_done", "y_added", "own_v", "own_p",
                 "group_loaded0", "group_loaded1")
        s = {n: sem(n) for n in names}
        lg_ps = PS[:, 1, 0:TT * E].rearrange("p (t e) -> p t e", t=TT)
        place_ps = PS[:, 1, 64:64 + TOP * TT * E].rearrange("p (k t e) -> p k t e", k=TOP, t=TT)
        block = ctx.enter_context(nc.Block())

        @block.sync
        def _(sync):
            sync.dma_start(wr[:, :, :], io["L2_ffn_w_router"].rearrange("(k p) e -> p k e", p=P)).then_inc(s["weights"], 16)

            def load(g, buf):
                done = s[f"group_loaded{buf}"]
                for e in range(EG):
                    at = g * EG + e
                    sync.dma_start(w_up[:, buf, e, 0, :, :], io["L2_ffn_w_gate"][at].rearrange("(k p) h -> p k h", p=P)).then_inc(done, 16)
                    sync.dma_start(w_up[:, buf, e, 1, :, :], io["L2_ffn_w_fc"][at].rearrange("(k p) h -> p k h", p=P)).then_inc(done, 16)
                    sync.dma_start(w_pr[:, buf, e, :], io["L2_ffn_w_proj"][at]).then_inc(done, 16)

            for g in range(NG):
                if g >= 2:
                    sync.wait_ge(s["down_done"], EG * (g - 1))
                load(g, g % 2)

        @block.tensor
        def _(pe):
            def turn_x(b, par):
                pe.wait_ge(s["xn_ready"], b + 1)
                turn_tokens(pe, PS[:, 0, :], xn[par], ident).then_inc(s["xT_turned"], 1)

            def turn(b, par, last):
                pe.wait_ge(s["xT_ready"], b + 1)
                for t in range(TT):
                    for k in range(KD):
                        mm = pe.matmul(lg_ps[:, t, :], xT[:, k, t * P:(t + 1) * P], wr[:, k, :], start=(k == 0), stop=(k == KD - 1))
                mm.then_inc(s["logits_done"], 1)
                if not last:
                    turn_x(b + 1, 1 - par)
                pe.wait_ge(s["choice_ready"], b + 1)
                for k in range(TOP):
                    for t in range(TT):
                        before = [(all_ones, 0, u) for u in range(TT)] if k else []
                        before += [(all_ones, k, u) for u in range(t)] + [(later_than, k, t)]
                        for n, (m, kk, u) in enumerate(before):
                            mm = pe.matmul(place_ps[:, k, t, :], m[:, :], oh[:, kk, u, :], start=(n == 0), stop=(n == len(before) - 1))
                mm.then_inc(s["place_done"], 1)
                pe.wait_ge(s["dispatch_ready"], b + 1)
                for c in range(KD):
                    for t in range(TT):
                        mm = pe.matmul(PS[:, 2 + c, :], xn[par][:, t, c * P:(c + 1) * P], Dm[:, t, :], start=(t == 0), stop=(t == TT - 1))
                mm.then_inc(s["dispatched"], 1)
                pe.wait_ge(s["collect_ready"], b + 1)
                for half in range(2):
                    for g in range(2):
                        for t in range(TT):
                            at = (2 * half + g) * P
                            mm = pe.transpose(PS[:, 4 + half, g * S + t * P:g * S + t * P + P], Wm[:, t, at:at + P], ident[:, :])
                    mm.then_inc(s[f"collect_turned{half}"], 1)

            def down(n):
                g, e = n // EG, n % EG
                pe.wait_ge(s["hidden_ready"], n + 1)
                if e == 0 and g:
                    pe.wait_ge(s["out_copied"], g)
                for b in range(B):
                    mm = pe.matmul(PS[e * CAP:(e + 1) * CAP, 4 + b // 2, (b % 2) * D:(b % 2) * D + D], hid[:, n % 2, b * CAP:(b + 1) * CAP],
                                   w_pr[:, g % 2, e, :], start=True, stop=True, tile_position=(0, e * CAP))
                mm.then_inc(s["down_done"], 1)

            pe.wait_ge(s["weights"], 16)
            turn_x(0, 0)
            in_pairs(pe, turn)

            for g in range(NG):
                pe.wait_ge(s[f"group_loaded{g % 2}"], 16 * 3 * EG * (g // 2 + 1))
                if g == 0:
                    pe.wait_ge(s["dispatched_copied"], B)
                for e in range(EG):
                    n = EG * g + e
                    if n >= 2:
                        pe.wait_ge(s["hidden_ready"], n - 1)
                    for which in range(2):
                        for k in range(KD):
                            mm = pe.matmul(PS[:, n % 2, which * S:(which + 1) * S], w_up[:, g % 2, e, which, k, :],
                                           xd[:, k, n, :, :].rearrange("p b c -> p (b c)"), start=(k == 0), stop=(k == KD - 1))
                    mm.then_inc(s["up_done"], 1)
                    if n >= 1:
                        down(n - 1)
            down(E - 1)

            for b in range(B):
                if b == 0:
                    pe.wait_ge(s["out_copied"], NG)
                if b >= 2:
                    pe.wait_ge(s["y_added"], b - 1)
                for t in range(TT):
                    for g in range(NG):
                        mm = pe.matmul(PS[:, b % 2, t * D:(t + 1) * D], WT[:, b, g, t * P:(t + 1) * P], out[:, g, b, :],
                                       start=(g == 0), stop=(g == NG - 1))
                mm.then_inc(s["y_done"], 1)

        @block.scalar
        def _(act):
            def turn(b, par, last):
                act.wait_ge(s["z_ready"], b + 1)
                act.activation(ez[:, :, :], lg[:, :, :], ACT.Exp).then_inc(s["exp_ready"], 1)
                if not last:
                    act.wait_ge(s["xT_turned"], b + 2)
                    act.activation(xT[:, :, :].rearrange("p k s -> p (k s)"), PS[:, 0, :], ACT.Copy).then_inc(s["xT_ready"], 1)
                act.wait_ge(s["dispatched"], b + 1)
                for c in range(KD):
                    i = act.activation(xd[:, c, :, b, :], PS[:, 2 + c, :].rearrange("p (e n) -> p e n", e=E), ACT.Copy)
                i.then_inc(s["dispatched_copied"], 1)

            act.wait_ge(s["xT_turned"], 1)
            act.activation(xT[:, :, :].rearrange("p k s -> p (k s)"), PS[:, 0, :], ACT.Copy).then_inc(s["xT_ready"], 1)
            in_pairs(act, turn)
            for n in range(E):
                act.wait_ge(s["up_done"], n + 1)
                act.activation(gate[:, n % 2, :], PS[:, n % 2, 0:S], ACT.Silu).then_inc(s["silu_ready"], 1)
                if n % EG == EG - 1:
                    act.wait_ge(s["down_done"], n + 1)
                    act.activation(out[:, n // EG, :, :].rearrange("p b d -> p (b d)"), PS[:, 4:8, :].rearrange("p n d -> p (n d)"),
                                   ACT.Copy).then_inc(s["out_copied"], 1)

        @block.gpsimd
        def _(pool):
            def turn(b, par, last):
                st = Steps(pool, s["own_p"], b * 2 * TT, 2 * TT)
                wait_apart(pool, s["slots_ready"], b + 1, apart_pool)
                for t in range(TT):
                    st.step(pool.tensor_scalar(Wm[:, t, :], iota[:, 0:SLOTS], got[:, 0, t:t + 1], prob[:, 0, t:t + 1], ALU.is_equal, ALU.mult), apart_pool)
                    st.step(pool.tensor_scalar(W2[:, t, :], iota[:, 0:SLOTS], got[:, 1, t:t + 1], prob[:, 1, t:t + 1], ALU.is_equal, ALU.mult), apart_pool)
                pool.tensor_tensor(Wm[:, :, :], Wm[:, :, :], W2[:, :, :], ALU.add).then_inc(s["collect_ready"], 1)
                st.end()
            in_pairs(pool, turn)

        @block.vector
        def _(dve):
            TURN = ROUTE_STEPS + 4 + 4 + TT

            def turn(b, par, last):
                st = Steps(dve, s["own_v"], LN_STEPS + b * (LN_STEPS + TURN), TURN + LN_STEPS * (not last))
                dve.wait_ge(s["logits_done"], b + 1)
                route(dve, st, E, lg_ps, None, rw, iota, s["z_ready"], s["exp_ready"], b, apart_v, s["choice_ready"])
                if not last:
                    layer_norm(dve, st, X, b * TT + TT, work, xn[1 - par], s["xn_ready"], apart_v)
                st.step(dve.tensor_tensor(tmp[:, :, :, :], oh[:, :, :, :], bc(ez[:, None, :, :], [P, TOP, TT, E]), ALU.mult))
                st.step(dve.tensor_reduce(prob[:, :, :], tmp[:, :, :, :], AX.X, ALU.add))
                dve.wait_ge(s["place_done"], b + 1)
                st.step(dve.tensor_tensor(tmp[:, :, :, :], place_ps, oh[:, :, :, :], ALU.mult))
                st.step(dve.tensor_reduce(place[:, :, :], tmp[:, :, :, :], AX.X, ALU.add))
                st.step(dve.tensor_scalar(got[:, :, :], place[:, :, :], float(CAP - 1), None, ALU.min))
                st.step(dve.tensor_scalar(slot[:, :, :], ixf[:, :, 0:TOP].rearrange("p t k -> p k t"), float(CAP), None, ALU.mult))
                st.step(dve.tensor_tensor(got[:, :, :], got[:, :, :], slot[:, :, :], ALU.add))
                st.step(dve.tensor_scalar(slot[:, :, :], place[:, :, :], float(CAP - 1), 4.0 * SLOTS, ALU.is_gt, ALU.mult))
                dve.tensor_tensor(slot[:, :, :], slot[:, :, :], got[:, :, :], ALU.add).then_inc(s["slots_ready"], 1)
                dve.wait_ge(s["slots_ready"], b + 1)
                for t in range(TT):
                    st.step(dve.tensor_scalar(Dm[:, t, :], iota[:, 0:SLOTS], slot[:, 0, t:t + 1], None, ALU.is_equal))
                for t in range(TT):
                    i = dve.scalar_tensor_tensor(Dm[:, t, :], iota[:, 0:SLOTS], slot[:, 1, t:t + 1], Dm[:, t, :], ALU.is_equal, ALU.add)
                i.then_inc(s["dispatch_ready"], 1)
                for half in range(2):
                    dve.wait_ge(s[f"collect_turned{half}"], b + 1)
                    dve.tensor_copy(WT[:, b, 2 * half:2 * half + 2, :], PS[:, 4 + half, :].rearrange("p (g l) -> p g l", g=2)
                                    ).then_inc(s["collect_copied"], 1)
                st.end()

            st = Steps(dve, s["own_v"], 0, LN_STEPS)
            layer_norm(dve, st, X, 0, work, xn[0], s["xn_ready"], apart_v)
            in_pairs(dve, turn)
            for n in range(E):
                dve.wait_ge(s["silu_ready"], n + 1)
                if n >= 2:
                    dve.wait_ge(s["down_done"], n - 1)
                dve.tensor_tensor(hid[:, n % 2, :], gate[:, n % 2, :], PS[:, n % 2, S:2 * S], ALU.mult).then_inc(s["hidden_ready"], 1)
            for b in range(B):
                dve.wait_ge(s["y_done"], b + 1)
                dve.tensor_tensor(X[:, b * TT:(b + 1) * TT, :], PS[:, b % 2, :].rearrange("p (t d) -> p t d", t=TT),
                                  X[:, b * TT:(b + 1) * TT, :], ALU.add).then_inc(s["y_added"], 1)


def phase_ffn1(nc, io, X, PS, ident, iota, apart):
    E, HP, NR = 8, 128, 64
    CAP = S // 8
    SLOTS = E * CAP
    EG, NG = P // CAP, SLOTS // P
    ROUNDS = CAP // 8
    TAKEN, NONE = -1e30, 4096.0
    QK_SCALE = float(HP) ** -0.5
    apart_v, apart_pool, apart_sync, apart_pe = apart
    with ExitStack() as ctx:
        sp = Space(nc, ctx, "f1")
        sb, sem = sp.sb, sp.sem
        wr = sb("w_router", [P, KD, E])
        w_qkv = sb("w_qkv", [P, 2, KD, 3 * HP])
        w_rot = sb("w_rot", [P, 2, KD, 2, NR])
        w_o = sb("w_o", [P, 2, D])
        table = sb("rope_table", [P, TT, HP + NR])
        mask = sb("mask", [P, P])
        work = ln_work(sb, "ln")
        xn = [sb(f"xn{i}", [P, TT, D]) for i in range(2)]
        xT = sb("xT", [P, KD, S])
        rank, top = sb("rank", [E, S]), sb("top", [E, 8])
        count, ones, slotv, sig = sb("count", [E, S]), sb("ones", [E, S]), sb("slot", [E, S]), sb("sigmoid", [E, S])
        tok = sb("by_token", [P, TT, 2, E])
        Dm, Wm = sb("dispatch", [P, TT, E, CAP]), sb("collect", [P, TT, E, CAP])
        xd = sb("x_dispatched", [P, KD, E, B, CAP])
        xe = sb("x_expert", [P, KD, B * CAP])
        cosd, sind = sb("cos_dispatched", [P, E, B, CAP]), sb("sin_dispatched", [NR, E, B, CAP])
        WT = sb("collectT", [P, B, NG, S])
        qT, kT, turned = sb("qT", [P, B * CAP]), sb("kT", [P, B * CAP]), sb("rotated", [NR, 2, B * CAP])
        v = sb("v", [P, 2, HP])
        sc, mx, nmx, den = sb("scores", [P, 2, P]), sb("row_max", [P, 2]), sb("neg_max", [P, 2]), sb("den", [P, 2])
        pr, prT, avT = sb("probs", [P, 2, P]), sb("probsT", [P, 2, P]), sb("avT", [P, B * CAP])
        out = sb("expert_out", [P, NG, B, D])
        names = ("weights", "xn_ready", "xT_turned", "xT_ready", "logits_done", "exp_ready", "slots_ready", "by_token_done",
                 "dispatch_ready", "dispatched", "dispatched_copied", "collect_ready", "collect_turned", "collect_copied",
                 "own_v", "loaded0", "loaded1", "projected", "v_ready", "qk_ready", "scores_done", "max_ready", "probs_ready", "scaled",
                 "probs_turned", "probsT_ready", "av_done", "av_ready", "down_done", "out_copied", "y_done", "y_added",
                 "rope_copied", "logits_copied", "xe_ready", "masked")
        s = {n: sem(n) for n in names}
        block = ctx.enter_context(nc.Block())
        lt_ps = PS[0:E, 1, 0:S]
        tok_ps = PS[:, 1, S:S + TT * 2 * E].rearrange("p (t a e) -> p t a e", t=TT, a=2)

        @block.sync
        def _(sync):
            sync.dma_start(wr[:, :, :], io["L1_ffn_WrT"].rearrange("(k p) e -> p k e", p=P)).then_inc(s["weights"], 16)
            sync.dma_start(table[:, :, :], io["rope_table"].rearrange("(t p) n -> p t n", p=P)).then_inc(s["weights"], 16)

            def load(e):
                done = s[f"loaded{e % 2}"]
                w = io["L1_ffn_Wqkv"][e].rearrange("(k p) (a n) -> p k a n", p=P, a=3)
                sync.dma_start(w_qkv[:, e % 2, :, :], io["L1_ffn_Wqkv"][e].rearrange("(k p) n -> p k n", p=P)).then_inc(done, 16)
                for half in range(2):
                    for a in range(2):
                        sync.dma_start(w_rot[:, e % 2, :, a, half * NR // 2:(half + 1) * NR // 2],
                                       w[:, :, a, (1 - half) * NR // 2:(2 - half) * NR // 2]).then_inc(done, 16)
                sync.dma_start(w_o[:, e % 2, :], io["L1_ffn_Wo"][e]).then_inc(done, 16)

            for e in range(E):
                if e >= 2:
                    sync.wait_ge(s["down_done"], e - 1)
                load(e)

        @block.gpsimd
        def _(pool):
            pool.memset(ones[:, :], 1.0).then_inc(s["masked"], 1)
            pool.memset(mask[:, :], 0.0).then_inc(s["masked"], 1)
            pool.wait_ge(s["masked"], 2)
            pool.affine_select(out=mask[:, :], in_=mask[:, :], compare_op=ALU.is_ge, fill=-1e30,
                               base=0, pattern=[[-1, P]], channel_multiplier=1).then_inc(s["masked"], 1)
            pool.wait_ge(s["masked"], 3)
            for g in range(1, EG):
                at = mask[:, 0:g * CAP]
                pool.affine_select(out=at, in_=at, compare_op=ALU.is_gt, fill=-1e30,
                                   base=g * CAP, pattern=[[0, g * CAP]], channel_multiplier=-1).then_inc(s["masked"], 1)
                pool.wait_ge(s["masked"], 3 + g)
            with pool.Fori(0, B) as b:
                pool.wait_ge(s["dispatch_ready"], b + 1)
                pool.tensor_tensor(Wm[:, :, :, :], Dm[:, :, :, :], bc(tok[:, :, 1, :, None], [P, TT, E, CAP]), ALU.mult
                                   ).then_inc(s["collect_ready"], 1)

        @block.tensor
        def _(pe):
            def turn_x(b, par):
                pe.wait_ge(s["xn_ready"], b + 1)
                turn_tokens(pe, PS[:, 0, :], xn[par], ident).then_inc(s["xT_turned"], 1)

            def turn(b, par, last):
                pe.wait_ge(s["xT_ready"], b + 1)
                for k in range(KD):
                    mm = pe.matmul(lt_ps, wr[:, k, :], xT[:, k, :], start=(k == 0), stop=(k == KD - 1))
                mm.then_inc(s["logits_done"], 1)
                if not last:
                    turn_x(b + 1, 1 - par)
                wait_apart(pe, s["slots_ready"], b + 1, apart_pe)
                for t in range(TT):
                    for a, src in enumerate((slotv, sig)):
                        mm = pe.transpose(tok_ps[:, t, a, :], src[:, t * P:(t + 1) * P], ident[0:E, 0:E])
                mm.then_inc(s["by_token_done"], 1)
                pe.wait_ge(s["dispatch_ready"], b + 1)
                D2 = [Dm[:, t, :, :].rearrange("p e c -> p (e c)") for t in range(TT)]
                for c in range(KD):
                    for t in range(TT):
                        mm = pe.matmul(PS[:, 2, c * SLOTS:(c + 1) * SLOTS], xn[par][:, t, c * P:(c + 1) * P], D2[t], start=(t == 0), stop=(t == TT - 1))
                for at, width in ((0, HP), (HP, NR)):
                    for t in range(TT):
                        mm = pe.matmul(PS[0:width, 3, 2 * at:2 * at + SLOTS], table[:, t, at:at + width], D2[t], start=(t == 0), stop=(t == TT - 1))
                mm.then_inc(s["dispatched"], 1)
                pe.wait_ge(s["collect_ready"], b + 1)
                for g in range(NG):
                    for t in range(TT):
                        mm = pe.transpose(PS[:, 4, g * S + t * P:g * S + t * P + P],
                                          Wm[:, t, g * EG:(g + 1) * EG, :].rearrange("p e c -> p (e c)"), ident[:, :])
                mm.then_inc(s["collect_turned"], 1)

            pe.wait_ge(s["weights"], 32)
            turn_x(0, 0)
            in_pairs(pe, turn)

            pe.wait_ge(s["dispatched_copied"], B)
            pe.wait_ge(s["rope_copied"], B)
            for e in range(E):
                wb = e % 2
                pe.wait_ge(s[f"loaded{wb}"], 16 * 6 * (e // 2 + 1))
                if e:
                    pe.wait_ge(s["qk_ready"], e)
                for a in range(2):
                    for k in range(KD):
                        pe.matmul(PS[:, 0, a * S:(a + 1) * S], w_qkv[:, wb, k, a * HP:(a + 1) * HP],
                                  xd[:, k, e, :, :].rearrange("p b c -> p (b c)"), start=(k == 0), stop=(k == KD - 1))
                    for k in range(KD):
                        mm = pe.matmul(PS[0:NR, 1, a * S:(a + 1) * S], w_rot[:, wb, k, a, :],
                                       xd[:, k, e, :, :].rearrange("p b c -> p (b c)"), start=(k == 0), stop=(k == KD - 1))
                for g in range(2):
                    for k in range(KD):
                        mm = pe.matmul(PS[:, 2, g * HP:(g + 1) * HP], xd[:, k, e, g * EG:(g + 1) * EG, :].rearrange("p b c -> p (b c)"),
                                       w_qkv[:, wb, k, 2 * HP:3 * HP], start=(k == 0), stop=(k == KD - 1))
                mm.then_inc(s["projected"], 1)
                pe.wait_ge(s["qk_ready"], e + 1)
                for g in range(2):
                    mm = pe.matmul(PS[:, 3, g * P:(g + 1) * P], qT[:, g * P:(g + 1) * P], kT[:, g * P:(g + 1) * P], start=True, stop=True)
                mm.then_inc(s["scores_done"], 1)
                pe.wait_ge(s["scaled"], e + 1)
                for g in range(2):
                    mm = pe.transpose(PS[:, 3, S + g * P:S + (g + 1) * P], pr[:, g, :], ident[:, :])
                mm.then_inc(s["probs_turned"], 1)
                pe.wait_ge(s["probsT_ready"], e + 1)
                pe.wait_ge(s["v_ready"], e + 1)
                for g in range(2):
                    mm = pe.matmul(PS[:, 2, S + g * P:S + (g + 1) * P], v[:, g, :], prT[:, g, :], start=True, stop=True)
                mm.then_inc(s["av_done"], 1)
                pe.wait_ge(s["av_ready"], e + 1)
                if e % EG == 0 and e:
                    pe.wait_ge(s["out_copied"], e // EG)
                r = (e % EG) * CAP
                for b in range(B):
                    mm = pe.matmul(PS[r:r + CAP, 4 + b // 2, (b % 2) * D:(b % 2) * D + D], avT[:, b * CAP:(b + 1) * CAP],
                                   w_o[:, wb, :], start=True, stop=True, tile_position=(0, r))
                mm.then_inc(s["down_done"], 1)

            for b in range(B):
                if b == 0:
                    pe.wait_ge(s["out_copied"], NG)
                if b >= 2:
                    pe.wait_ge(s["y_added"], b - 1)
                for t in range(TT):
                    for g in range(NG):
                        mm = pe.matmul(PS[:, b % 2, t * D:(t + 1) * D], WT[:, b, g, t * P:(t + 1) * P], out[:, g, b, :],
                                       start=(g == 0), stop=(g == NG - 1))
                mm.then_inc(s["y_done"], 1)

        @block.scalar
        def _(act):
            def copy_x():
                return act.activation(xT[:, :, :].rearrange("p k s -> p (k s)"), PS[:, 0, :], ACT.Copy)

            def turn(b, par, last):
                act.wait_ge(s["logits_copied"], b + 1)
                act.activation(sig[:, :], count[:, :], ACT.Exp, scale=-1.0).then_inc(s["exp_ready"], 1)
                if not last:
                    act.wait_ge(s["xT_turned"], b + 2)
                    copy_x().then_inc(s["xT_ready"], 1)
                act.wait_ge(s["dispatched"], b + 1)
                act.activation(xd[:, 0, :, b, :], PS[:, 2, 0:SLOTS].rearrange("p (e n) -> p e n", e=E), ACT.Copy)
                act.activation(xd[:, 1, :, b, :], PS[:, 2, SLOTS:2 * SLOTS].rearrange("p (e n) -> p e n", e=E), ACT.Copy
                               ).then_inc(s["dispatched_copied"], 1)
                act.activation(cosd[:, :, b, :], PS[:, 3, 0:SLOTS].rearrange("p (e n) -> p e n", e=E), ACT.Copy)
                act.activation(sind[:, :, b, :], PS[0:NR, 3, SLOTS:2 * SLOTS].rearrange("p (e n) -> p e n", e=E), ACT.Copy
                               ).then_inc(s["rope_copied"], 1)

            act.wait_ge(s["xT_turned"], 1)
            copy_x().then_inc(s["xT_ready"], 1)
            in_pairs(act, turn)
            for e in range(E):
                act.wait_ge(s["projected"], e + 1)
                if e:
                    act.wait_ge(s["av_done"], e)
                act.activation(v[:, :, :].rearrange("p g n -> p (g n)"), PS[:, 2, 0:S], ACT.Copy).then_inc(s["v_ready"], 1)
                act.wait_ge(s["max_ready"], e + 1)
                for g in range(2):
                    i = act.activation(pr[:, g, :], sc[:, g, :], ACT.Exp, bias=nmx[:, g:g + 1], scale=QK_SCALE, accum_out=den[:, g:g + 1])
                i.then_inc(s["probs_ready"], 1)
                act.wait_ge(s["probs_turned"], e + 1)
                act.activation(prT[:, :, :].rearrange("p g n -> p (g n)"), PS[:, 3, S:2 * S], ACT.Copy).then_inc(s["probsT_ready"], 1)
                act.wait_ge(s["av_done"], e + 1)
                act.activation(avT[:, :], PS[:, 2, S:2 * S], ACT.Copy).then_inc(s["av_ready"], 1)
                if e % EG == EG - 1:
                    act.wait_ge(s["down_done"], e + 1)
                    act.activation(out[:, e // EG, :, :].rearrange("p b d -> p (b d)"), PS[:, 4:8, :].rearrange("p n d -> p (n d)"),
                                   ACT.Copy).then_inc(s["out_copied"], 1)

        @block.vector
        def _(dve):
            TURN = 1 + 2 * ROUNDS + 4 + 1 + 1

            def turn(b, par, last):
                st = Steps(dve, s["own_v"], LN_STEPS + b * (LN_STEPS + TURN), TURN + LN_STEPS * (not last))
                dve.wait_ge(s["logits_done"], b + 1)
                dve.tensor_copy(count[:, :], lt_ps).then_inc(s["logits_copied"], 1)
                dve.wait_ge(s["logits_copied"], b + 1)
                st.step(dve.tensor_scalar(rank[:, :], count[:, :], 17.0, None, ALU.min), apart_v)
                for _ in range(ROUNDS):
                    st.step(dve.max(top[:, :], rank[:, :]), apart_v)
                    st.step(dve.match_replace(rank[:, :], top[:, :], rank[:, :], TAKEN), apart_v)
                st.step(dve.tensor_scalar(rank[:, :], rank[:, :], TAKEN / 2, None, ALU.is_le))
                dve.wait_ge(s["exp_ready"], b + 1)
                st.step(dve.tensor_tensor_scan(count[:, :], ones[:, :], rank[:, :], 0.0, ALU.mult, ALU.add))
                st.step(dve.scalar_tensor_tensor(slotv[:, :], rank[:, :], -NONE, count[:, :], ALU.mult, ALU.add))
                st.step(dve.tensor_scalar(sig[:, :], sig[:, :], 1.0, None, ALU.add))
                dve.tensor_scalar(slotv[:, :], slotv[:, :], NONE - 1.0, None, ALU.add)
                dve.reciprocal(sig[:, :], sig[:, :]).then_inc(s["slots_ready"], 1)
                if not last:
                    layer_norm(dve, st, X, b * TT + TT, work, xn[1 - par], s["xn_ready"], apart_v)
                dve.wait_ge(s["by_token_done"], b + 1)
                st.step(dve.tensor_copy(tok[:, :, :, :], tok_ps))
                for t in range(TT):
                    i = dve.tensor_tensor(Dm[:, t, :, :], bc(iota[:, None, 0:CAP], [P, E, CAP]), bc(tok[:, t, 0, :, None], [P, E, CAP]), ALU.is_equal)
                i.then_inc(s["dispatch_ready"], 1)
                dve.wait_ge(s["collect_turned"], b + 1)
                st.step(dve.tensor_copy(WT[:, b, :, :], PS[:, 4, :].rearrange("p (g l) -> p g l", g=NG)))
                st.end()

            st = Steps(dve, s["own_v"], 0, LN_STEPS)
            dve.wait_ge(s["masked"], 2 + EG)
            layer_norm(dve, st, X, 0, work, xn[0], s["xn_ready"], apart_v)
            in_pairs(dve, turn)
            st = Steps(dve, s["own_v"], B * (LN_STEPS + TURN), E * 7)
            dve.wait_ge(s["rope_copied"], B)
            for e in range(E):
                dve.wait_ge(s["projected"], e + 1)
                if e:
                    dve.wait_ge(s["scores_done"], e)
                ce, se = cosd[:, e, :, :].rearrange("p b c -> p (b c)"), sind[:, e, :, :].rearrange("p b c -> p (b c)")
                for a, dst in enumerate((qT, kT)):
                    st.step(dve.tensor_tensor(dst[:, :], PS[:, 0, a * S:(a + 1) * S], ce, ALU.mult))
                    st.step(dve.tensor_tensor(turned[:, a, :], PS[0:NR, 1, a * S:(a + 1) * S], se, ALU.mult))
                for a, dst in enumerate((qT, kT)):
                    i = dve.tensor_tensor(dst[0:NR, :], dst[0:NR, :], turned[:, a, :], ALU.add)
                i.then_inc(s["qk_ready"], 1)
                dve.wait_ge(s["scores_done"], e + 1)
                st.step(dve.tensor_tensor(sc[:, :, :], PS[:, 3, 0:S].rearrange("p (g n) -> p g n", g=2), bc(mask[:, None, :], [P, 2, P]), ALU.add))
                st.step(dve.tensor_reduce(mx[:, :], sc[:, :, :], AX.X, ALU.max))
                dve.tensor_scalar(nmx[:, :], mx[:, :], -QK_SCALE, None, ALU.mult).then_inc(s["max_ready"], 1)
                dve.wait_ge(s["probs_ready"], e + 1)
                st.step(dve.reciprocal(den[:, :], den[:, :]))
                dve.tensor_tensor(pr[:, :, :], pr[:, :, :], bc(den[:, :, None], [P, 2, P]), ALU.mult).then_inc(s["scaled"], 1)
            st.end()
            for b in range(B):
                dve.wait_ge(s["y_done"], b + 1)
                dve.tensor_tensor(X[:, b * TT:(b + 1) * TT, :], PS[:, b % 2, :].rearrange("p (t d) -> p t d", t=TT),
                                  X[:, b * TT:(b + 1) * TT, :], ALU.add).then_inc(s["y_added"], 1)


MH, MHD = 8, 32
MK = P // MHD
HOPS = S + P


def phase_hops(nc, io, X, CT, PS, ident, apart, qT, hop):
    RING = 4
    CH = 16
    apart_v, apart_pool, apart_sync, apart_pe = apart
    with ExitStack() as ctx:
        sp = Space(nc, ctx, "h0")
        sb, sem = sp.sb, sp.sem
        idx = sb("idx", [P, HOPS], U32)
        idx_now = sb("idx_now", [P, 2, CH], U32)
        rows = sb("rows", [P, RING, 4, D])
        rowsT = sb("rowsT", [P, 2, KD, 4 * P])
        q_bd = sb("q_block_diagonal", [P, 2, KD, CH, MK, B])
        work = ln_work(sb, "ln")
        xn = sb("xn", [P, TT, D])
        names = ("xn_ready", "xT_turned", "qT_ready", "own_v", "own_p", "own_a", "idx_loaded", "idx_ready", "turned", "half0_copied", "half1_copied",
                 "multiplied", "hop_copied", "q_ready", "zeroed", "gathered0", "gathered1", "gathered2", "gathered3")
        s = {n: sem(n) for n in names}
        block = ctx.enter_context(nc.Block())

        def chunks(eng, chunk):
            with eng.Fori(0, S // (2 * CH)) as i:
                for half in range(2):
                    chunk(2 * i + half, (2 * i + half) * CH, (2 * i + half) * CH, half)
            with eng.Fori(S // (2 * CH), HOPS // (2 * CH)) as i:
                for half in range(2):
                    chunk(2 * i + half, (2 * i + half) * CH - P, (2 * i + half) * CH, half)

        @block.sync
        def _(sync):
            sync.dma_start(idx[:, 0:S], io["itokT"][0:P, :]).then_inc(s["idx_loaded"], 16)
            sync.dma_start(idx[:, S:HOPS], io["itokT"][P:S, P:S]).then_inc(s["idx_loaded"], 16)

        @block.gpsimd
        def _(pool):
            pool.wait_ge(s["idx_loaded"], 32)
            for c in range(2):
                pool.memset(q_bd[:, c, :, :, :, :], 0.0).then_inc(s["zeroed"], 1)

            def gather(c, half, peeled):
                if not peeled:
                    wait_apart(pool, s["turned"], 4 * c - 4, apart_pool)
                pool.tensor_copy(idx_now[:, half, :], idx[:, bass.ds(c * CH, CH)]).then_inc(s["idx_ready"], 1)
                wait_apart(pool, s["idx_ready"], c + 1, apart_pool)
                for g in range(4):
                    if not peeled:
                        wait_apart(pool, s["turned"], 4 * c + g - RING + 1, apart_pool)
                    for j in range(4):
                        pool.indirect_dma_start(
                            out=rows[:, g, j, :], out_offset=None, in_=io["L0_xattn_rpe"],
                            in_offset=bass.IndirectOffsetOnAxis(ap=idx_now[:, half, 4 * g + j:4 * g + j + 1], axis=0),
                        ).then_inc(s[f"gathered{g}"], 16)

            gather(0, 0, True)
            gather(1, 1, False)
            with pool.Fori(1, HOPS // (2 * CH)) as i:
                for half in range(2):
                    gather(2 * i + half, half, False)

        @block.tensor
        def _(pe):
            with pe.Fori(0, B) as b:
                pe.wait_ge(s["xn_ready"], b + 1)
                pe.wait_ge(s["qT_ready"], b)
                turn_tokens(pe, PS[:, 6, :], xn, ident).then_inc(s["xT_turned"], 1)

            def turn_rows(n, g):
                pe.wait_ge(s[f"gathered{g}"], 64 * n[1] + 64)
                for k in range(KD):
                    if not (isinstance(n[0], int) and n[0] < 2):
                        pe.wait_ge(s[f"half{k}_copied"], n[0] - 1)
                    for j in range(4):
                        mm = pe.transpose(PS[:, 2 * (g % 2) + k, j * P:(j + 1) * P], rows[:, g, j, k * P:(k + 1) * P], ident[:, :])
                mm.then_inc(s["turned"], 1)

            def multiply(n, g, half):
                if g == 0:
                    pe.wait_ge(s["q_ready"], n[1] + 1)
                for k in range(KD):
                    pe.wait_ge(s[f"half{k}_copied"], n[0] + 1)
                if not (isinstance(n[0], int) and n[0] < 2):
                    pe.wait_ge(s["hop_copied"], n[0] - 1)
                for j in range(4):
                    for k in range(KD):
                        mm = pe.matmul(PS[:, 4 + g % 2, (2 * j + k) * MK * B:(2 * j + k + 1) * MK * B], rowsT[:, g % 2, k, j * P:(j + 1) * P],
                                       q_bd[:, half, k, 4 * g + j, :, :].rearrange("p h b -> p (h b)"), start=True, stop=True)
                mm.then_inc(s["multiplied"], 1)

            def chunk(c, v0, T0, half, first=False):
                for g in range(4):
                    turn_rows((4 * c + g, c), g)
                    if g:
                        multiply((4 * c + g - 1, c), g - 1, half)
                    elif not first:
                        multiply((4 * c - 1, c - 1), 3, 1 - half)
            chunk(0, 0, 0, 0, True)
            chunk(1, 0, 0, 1)
            with pe.Fori(1, HOPS // (2 * CH)) as i:
                for half in range(2):
                    chunk(2 * i + half, 0, 0, half)
            last = HOPS // CH
            multiply((4 * last - 1, last - 1), 3, 1)

        @block.scalar
        def _(act):
            with act.Fori(0, B) as b:
                act.wait_ge(s["xT_turned"], b + 1)
                act.activation(qT[:, :, bass.ds(b * S, S)], PS[:, 6, :].rearrange("p (k s) -> p k s", k=KD), ACT.Copy).then_inc(s["qT_ready"], 1)
            act.wait_ge(s["zeroed"], 2)
            act.wait_ge(s["qT_ready"], B)

            def build(c, v0, half):
                if not (isinstance(c, int) and c < 2):
                    act.wait_ge(s["multiplied"], 4 * c - 4)
                for k in range(KD):
                    for h in range(MK):
                        r = slice(h * MHD, (h + 1) * MHD)
                        src = qT[r, k, :].rearrange("p (b v) -> p v b", b=B)[:, bass.ds(v0, CH), :]
                        i = act.activation(q_bd[r, half, k, :, h, :], src, ACT.Copy)
                i.then_inc(s["q_ready"], 1)

            build(0, 0, 0)
            build(1, CH, 1)

            def chunk(c, v0, T0, half, build_next=True):
                for g in range(4):
                    act.wait_ge(s["turned"], 4 * c + g + 1)
                    if not (isinstance(c, int) and 4 * c + g < 2):
                        act.wait_ge(s["multiplied"], 4 * c + g - 1)
                    act.activation(rowsT[:, g % 2, 1, :], PS[:, 2 * (g % 2) + 1, :], ACT.Copy).then_inc(s["half1_copied"], 1)
                if build_next:
                    build(c + 2, build_next(c + 2), half)
            low, high = (lambda c: c * CH), (lambda c: c * CH - P)
            for half in range(2):
                chunk(half, 0, 0, half, low)
            with act.Fori(1, S // (2 * CH) - 1) as i:
                for half in range(2):
                    chunk(2 * i + half, 0, 0, half, low)
            with act.Fori(S // (2 * CH) - 1, HOPS // (2 * CH) - 1) as i:
                for half in range(2):
                    chunk(2 * i + half, 0, 0, half, high)
            for half in range(2):
                chunk(HOPS // CH - 2 + half, 0, 0, half, None)

        @block.vector
        def _(dve):
            with dve.Fori(0, B) as b:
                st = Steps(dve, s["own_v"], b * LN_STEPS, LN_STEPS)
                dve.wait_ge(s["xT_turned"], b)
                layer_norm(dve, st, X, b * TT, work, xn, s["xn_ready"], apart_v)
                st.end()

            def chunk(c, half):
                first = isinstance(c, int) and c == 0
                for g in range(4):
                    dve.wait_ge(s["turned"], 4 * c + g + 1)
                    if not (first and g < 2):
                        dve.wait_ge(s["multiplied"], 4 * c + g - 1)
                    dve.tensor_copy(rowsT[:, g % 2, 0, :], PS[:, 2 * (g % 2), :]).then_inc(s["half0_copied"], 1)
                    if not (first and g == 0):
                        take(c, g - 1)

            def take(c, g):
                dve.wait_ge(s["multiplied"], 4 * c + g + 1)
                dve.tensor_copy(hop[:, bass.ds(c * CH + 4 * g, 4), :], PS[:, 4 + g % 2, 0:4 * MH * B].rearrange("p (j n) -> p j n", j=4)
                                ).then_inc(s["hop_copied"], 1)
            chunk(0, 0)
            chunk(1, 1)
            with dve.Fori(1, HOPS // (2 * CH)) as i:
                for half in range(2):
                    chunk(2 * i + half, half)
            take(HOPS // CH - 1, 3)


def phase_mlstm(nc, io, X, C, CT, PS, ident, identb, apart):
    with ExitStack() as ctx:
        qT = ctx.enter_context(nc.sbuf_tensor("x0_qT", [P, KD, B * S], F32))
        hop = ctx.enter_context(nc.sbuf_tensor("x0_hop", [P, HOPS, MH * B], F32))
        phase_hops(nc, io, X, CT, PS, ident, apart, qT, hop)
        mlstm_heads(nc, io, X, C, CT, PS, ident, identb, apart, qT, hop)


def mlstm_heads(nc, io, X, C, CT, PS, ident, identb, apart, qT, hop):
    GATES, FROW = 6, 32
    apart_v, apart_pool, apart_sync, apart_pe = apart
    with ExitStack() as ctx:
        sp = Space(nc, ctx, "m0")
        sb, sem = sp.sb, sp.sem
        wg = sb("w_gates", [P, GATES, FROW + MH])
        gbias = sb("gate_bias", [MH, 2])
        lnw, lnb = sb("ln_w", [P, D]), sb("ln_b", [P, D])
        sel = sb("head_rows", [MH, MH, P])
        mask = sb("mask", [P, P], BF16)
        ones = sb("ones", [MH, S])
        z, a, F, g = (sb(n, [MH, S]) for n in ("forget", "forget_abs", "F", "g"))
        zero = sb("zero", [MH, S])
        negG = [sb(f"negG{i}", [MH, S]) for i in range(2)]
        G, FG = sb("G", [MH, S]), sb("FG", [MH, S])
        tok = [sb(f"by_token{i}", [P, TT, 2, MH]) for i in range(2)]
        qm = sb("q_masked", [P, KD, MK, S])
        kT = sb("kT", [P, KD, S])
        Dd, A, Ct = (sb(n, [P, 2, HOPS]) for n in ("decay", "logits", "weights_"))
        one_col = sb("one_col", [P, 1])
        h, sq = sb("h", [P, TT, MH, MHD]), sb("h2", [P, TT, MH, MHD])
        n1, mu, ve, y, u = (sb(n, [P, TT, MH]) for n in ("norm", "mu", "var", "rstd", "u"))
        names = ("weights", "consts", "gates_done", "abs_ready", "ln_ready", "rows_ready", "by_token_done", "by_token_ready", "exps_ready",
                 "logits_done", "decay_done", "decay_ready", "summed", "multiplied", "pv_done", "h_taken", "qm_ready", "kT_ready", "own_v", "own_a", "w1", "negG_ready")
        s = {n: sem(n) for n in names}
        block = ctx.enter_context(nc.Block())
        U = PS[:, 6:8, 0:D].rearrange("p t (h d) -> p t h d", h=MH)
        SUM = PS[:, 6:8, D:D + MH]

        @block.sync
        def _(sync):
            for name, at in (("L0_xattn_igate_wT", 0), ("L0_xattn_fgate_wT", FROW)):
                sync.dma_start(wg[:, :, at:at + MH], io[name].rearrange("(k p) e -> p k e", p=P)).then_inc(s["weights"], 16)
            for n, name in enumerate(("L0_xattn_igate_b", "L0_xattn_fgate_b")):
                sync.dma_start(gbias[:, n:n + 1], io[name].rearrange("(e a) -> e a", a=1)).then_inc(s["weights"], 16)
            for tile, name in ((lnw, "L0_xattn_ln_w"), (lnb, "L0_xattn_ln_b")):
                sync.dma_start(tile[:, :], io[name].rearrange("(a n) -> a n", a=1).to_broadcast([P, D])).then_inc(s["weights"], 16)

        @block.gpsimd
        def _(pool):
            steps = [0]

            def const(i):
                steps[0] += 1
                i.then_inc(s["consts"], 1)
                pool.wait_ge(s["consts"], steps[0])

            const(pool.memset(wg[:, :, MH:FROW], 0.0))
            const(pool.memset(ones[:, :], 1.0))
            const(pool.memset(zero[:, :], 0.0))
            const(pool.memset(one_col[:, :], 1.0))
            const(pool.memset(sel[:, :, :], 0.0))
            const(pool.affine_select(out=sel[:, :, :], in_=sel[:, :, :], compare_op=ALU.not_equal, fill=1.0,
                                     base=0, pattern=[[-1, MH], [0, P]], channel_multiplier=1))
            const(pool.memset(mask[:, :], 0.0))
            const(pool.affine_select(out=mask[:, :], in_=mask[:, :], compare_op=ALU.is_ge, fill=-1e30,
                                     base=0, pattern=[[1, P]], channel_multiplier=-1))
            const(pool.memset(qm[:, :, :, :], 0.0))

            def spread(b, k):
                for n in range(MK):
                    r = slice(n * MHD, (n + 1) * MHD)
                    pool.tensor_copy(qm[r, k, n, :], qT[r, k, bass.ds(b * S, S)]).then_inc(s["qm_ready"], 1)
                pool.wait_ge(s["qm_ready"], MK * (KD * b + k + 1))

            def turn(b, par, last):
                for n in range(MH):
                    pool.wait_ge(s["decay_ready"], b * MH + n + 1)
                    pool.sem_inc(apart_pool, 1)
                    pool.wait_ge(s["summed"], b * MH + n + 1)
                    pool.tensor_tensor(Ct[:, n % 2, :], A[:, n % 2, :], Dd[:, n % 2, :], ALU.mult).then_inc(s["multiplied"], 1)
                    if not last and n % MK == MK - 1:
                        pool.wait_ge(s["multiplied"], b * MH + n + 1)
                        spread(b + 1, n // MK)
            for k in range(KD):
                spread(0, k)
            in_pairs(pool, turn)

        @block.tensor
        def _(pe):
            def gates(b):
                for kk in range(GATES):
                    src = qT if kk < KD else CT
                    mm = pe.matmul(PS[0:FROW + MH, 4, 0:S], wg[:, kk, :], src[:, kk % KD, bass.ds(b * S, S)], start=(kk == 0), stop=(kk == GATES - 1))
                mm.then_inc(s["gates_done"], 1)

            def turn_rows(b):
                wait_apart(pe, s["rows_ready"], b + 1, apart_pe)
                for t in range(TT):
                    for n, src in enumerate((g, FG)):
                        mm = pe.transpose(PS[:, 5, (2 * t + n) * MH:(2 * t + n + 1) * MH], src[:, t * P:(t + 1) * P], ident[0:MH, 0:MH])
                mm.then_inc(s["by_token_done"], 1)

            def pv(b, n):
                if n == 0:
                    pe.wait_ge(s["h_taken"], b)
                pe.wait_ge(s["multiplied"], b * MH + n + 1)
                parts = [(0, 0, 0), (1, P, 0), (1, S, 1)]
                for q, at, m in parts:
                    pe.matmul(PS[:, 6 + q, n * MHD:(n + 1) * MHD], Ct[:, n % 2, at:at + P], C[:, bass.ds(b * TT + m, 1), n * MHD:(n + 1) * MHD],
                              start=(at != S), stop=(at != P))
                for q, at, m in parts:
                    mm = pe.matmul(PS[:, 6 + q, D + n:D + n + 1], Ct[:, n % 2, at:at + P], one_col[:, :], start=(at != S), stop=(at != P))
                mm.then_inc(s["pv_done"], 1)

            def turn(b, par, last):
                if not last:
                    gates(b + 1)
                for n in range(MH):
                    k = n // MK
                    if n % MK == 0:
                        pe.wait_ge(s["qm_ready"], MK * (KD * b + k + 1))
                        pe.wait_ge(s["kT_ready"], KD * b + k + 1)
                    if n >= 2:
                        pe.wait_ge(s["summed"], b * MH + n - 1)
                        pe.wait_ge(s["decay_ready"], b * MH + n - 1)
                    pe.matmul(PS[:, 2 + n % 2, 0:S], kT[:, k, 0:P], qm[:, k, n % MK, :], start=True, stop=True)
                    pe.matmul(PS[:, 2 + n % 2, S:HOPS], kT[:, k, P:S], qm[:, k, n % MK, P:S], start=True, stop=True).then_inc(s["logits_done"], 1)
                    if n == 0:
                        wait_apart(pe, s["negG_ready"], b + 1, apart_pe)
                    pe.matmul(PS[:, n % 2, 0:S], sel[:, n, :], negG[par][:, :], start=True, stop=False)
                    pe.matmul(PS[:, n % 2, 0:P], identb[:, :], mask[:, :], start=False, stop=True)
                    pe.matmul(PS[:, n % 2, S:HOPS], sel[:, n, :], negG[par][:, P:S], start=True, stop=False)
                    pe.matmul(PS[:, n % 2, S:HOPS], identb[:, :], mask[:, :], start=False, stop=True).then_inc(s["decay_done"], 1)
                    if n:
                        pv(b, n - 1)
                    if n == 5 and not last:
                        turn_rows(b + 1)
                pv(b, MH - 1)

            pe.wait_ge(s["weights"], 96)
            pe.wait_ge(s["consts"], 9)
            gates(0)
            turn_rows(0)
            in_pairs(pe, turn)

        @block.scalar
        def _(act):
            def keys(b, k):
                act.activation(kT[:, k, :], CT[:, k, bass.ds(b * S, S)], ACT.Copy, scale=float(MHD) ** -0.5).then_inc(s["kT_ready"], 1)

            def log_forget(b):
                act.wait_ge(s["abs_ready"], b + 1)
                act.activation(a[:, :], a[:, :], ACT.Exp, scale=-1.0).then_inc(s["own_a"], 1)
                act.wait_ge(s["own_a"], b + 1)
                act.activation(a[:, :], a[:, :], ACT.Ln, bias=1.0).then_inc(s["ln_ready"], 1)

            def by_token(b, par):
                act.wait_ge(s["by_token_done"], b + 1)
                ps = PS[:, 5, 0:TT * 2 * MH].rearrange("p (t n e) -> p t n e", t=TT, n=2)
                act.activation(tok[par][:, :, 0, :], ps[:, :, 0, :], ACT.Copy)
                act.activation(tok[par][:, :, 1, :], ps[:, :, 1, :], ACT.Exp, scale=-1.0).then_inc(s["by_token_ready"], 1)

            def turn(b, par, last):
                act.wait_ge(s["by_token_ready"], b + 1)
                for n in range(MH):
                    act.wait_ge(s["decay_done"], b * MH + n + 1)
                    act.wait_ge(s["multiplied"], b * MH + max(n - 1, 0))
                    act.activation(Dd[:, n % 2, 0:S], PS[:, n % 2, 0:S], ACT.Exp, bias=tok[par][:, 0, 0, n:n + 1])
                    act.activation(Dd[:, n % 2, S:HOPS], PS[:, n % 2, S:HOPS], ACT.Exp, bias=tok[par][:, 1, 0, n:n + 1]).then_inc(s["decay_ready"], 1)
                    if not last:
                        if n == 1:
                            log_forget(b + 1)
                        if n % MK == MK - 1:
                            act.wait_ge(s["logits_done"], b * MH + n + 1)
                            keys(b + 1, n // MK)
                        if n == 6:
                            by_token(b + 1, 1 - par)
            for k in range(KD):
                keys(0, k)
            log_forget(0)
            by_token(0, 0)
            in_pairs(act, turn)

        @block.vector
        def _(dve):
            ROW_STEPS, POST_STEPS = 2 + 4, 5 + 6 + 2 + 12 + 4

            def forget_abs(st, b):
                dve.wait_ge(s["gates_done"], b + 1)
                st.step(dve.tensor_scalar(g[:, :], PS[0:MH, 4, 0:S], gbias[:, 0:1], None, ALU.add))
                st.step(dve.tensor_scalar(z[:, :], PS[FROW:FROW + MH, 4, 0:S], gbias[:, 1:2], None, ALU.add))
                dve.scalar_tensor_tensor(a[:, :], z[:, :], -1.0, z[:, :], ALU.mult, ALU.max).then_inc(s["abs_ready"], 1)

            def rows(st, b, par):
                dve.wait_ge(s["ln_ready"], b + 1)
                st.step(dve.scalar_tensor_tensor(z[:, :], z[:, :], 0.0, a[:, :], ALU.min, ALU.subtract))
                st.step(dve.tensor_tensor_scan(F[:, :], ones[:, :], z[:, :], 0.0, ALU.mult, ALU.add))
                st.step(dve.tensor_tensor(g[:, :], g[:, :], F[:, :], ALU.subtract))
                st.step(dve.tensor_tensor_scan(G[:, :], g[:, :], zero[:, :], -3e38, ALU.max, ALU.add))
                dve.tensor_scalar(negG[par][:, :], G[:, :], -1.0, None, ALU.mult).then_inc(s["negG_ready"], 1)
                dve.tensor_tensor(FG[:, :], G[:, :], F[:, :], ALU.add).then_inc(s["rows_ready"], 1)

            def turn(b, par, last):
                st = Steps(dve, s["own_v"], ROW_STEPS + b * (ROW_STEPS + POST_STEPS), POST_STEPS + ROW_STEPS * (not last))
                for n in range(MH):
                    dve.wait_ge(s["logits_done"], b * MH + n + 1)
                    dve.wait_ge(s["multiplied"], b * MH + max(n - 1, 0))
                    dve.tensor_tensor(A[:, n % 2, :], PS[:, 2 + n % 2, 0:HOPS], hop[:, :, bass.ds(n * B + b, 1)], ALU.add).then_inc(s["summed"], 1)
                    if not last:
                        if n == 0:
                            forget_abs(st, b + 1)
                        if n == 3:
                            rows(st, b + 1, 1 - par)
                dve.wait_ge(s["pv_done"], b * MH + MH)
                st.step(dve.tensor_copy(n1[:, :, :], SUM))
                st.step(dve.scalar_tensor_tensor(n1[:, :, :], n1[:, :, :], -1.0, n1[:, :, :], ALU.mult, ALU.max))
                st.step(dve.tensor_tensor(n1[:, :, :], n1[:, :, :], tok[par][:, :, 1, :], ALU.max))
                st.step(dve.tensor_scalar(n1[:, :, :], n1[:, :, :], 1e-6, None, ALU.add))
                st.step(dve.reciprocal(n1[:, :, :], n1[:, :, :]))
                full = [P, TT, MH, MHD]
                dve.tensor_tensor(h[:, :, :, :], U, bc(n1[:, :, :, None], full), ALU.mult).then_inc(s["h_taken"], 1)
                dve.wait_ge(s["h_taken"], b + 1)
                st.step(dve.tensor_reduce(mu[:, :, :], h[:, :, :, :], AX.X, ALU.add))
                st.step(dve.tensor_scalar(mu[:, :, :], mu[:, :, :], 1.0 / MHD, None, ALU.mult))
                st.step(dve.tensor_tensor(h[:, :, :, :], h[:, :, :, :], bc(mu[:, :, :, None], full), ALU.subtract))
                st.step(dve.tensor_tensor(sq[:, :, :, :], h[:, :, :, :], h[:, :, :, :], ALU.mult))
                st.step(dve.tensor_reduce(ve[:, :, :], sq[:, :, :, :], AX.X, ALU.add))
                st.step(dve.tensor_scalar(ve[:, :, :], ve[:, :, :], 1.0 / MHD, LN_EPS, ALU.mult, ALU.add))
                rsqrt(st, dve, ve[:, :, :], y[:, :, :], u[:, :, :])
                st.step(dve.tensor_tensor(h[:, :, :, :], h[:, :, :, :], bc(y[:, :, :, None], full), ALU.mult))
                flat = h[:, :, :, :].rearrange("p t h d -> p t (h d)")
                st.step(dve.tensor_tensor(flat, flat, bc(lnw[:, None, :], [P, TT, D]), ALU.mult))
                st.step(dve.tensor_tensor(flat, flat, bc(lnb[:, None, :], [P, TT, D]), ALU.add))
                st.step(dve.tensor_tensor(X[:, bass.ds(b * TT, TT), :], X[:, bass.ds(b * TT, TT), :], flat, ALU.add))
                st.end()

            dve.wait_ge(s["weights"], 96)
            dve.wait_ge(s["consts"], 9)
            dve.tensor_scalar(lnw[:, :], lnw[:, :], 1.0, None, ALU.add).then_inc(s["w1"], 1)
            dve.wait_ge(s["w1"], 1)
            st = Steps(dve, s["own_v"], 0, ROW_STEPS)
            forget_abs(st, 0)
            rows(st, 0, 0)
            st.end()
            in_pairs(dve, turn)


SLOT_TILES = 2 * B * TT + 16 - 1


def phase_ffn3(nc, io, X, PS, ident, iota, apart, later_than, all_ones, slots_zeroed):
    E, H, TOP, NTOK = 16, 256, 2, B * TT
    NT = SLOT_TILES
    NG = (NT + 1) // 2
    RING = 4
    apart_v, apart_pool, apart_sync, apart_pe = apart
    slots_in, slots_out = io["slots_in"], io["slots_out"]
    with ExitStack() as ctx:
        sp = Space(nc, ctx, "f3")
        sb, sem = sp.sb, sp.sem
        wr = sb("w_gate", [P, KD, E])
        w12 = sb("w1_w2", [P, E, KD, 2, H])
        wc = sb("wc", [P, E, KD, D])
        work = ln_work(sb, "ln")
        xn = [sb(f"xn{i}", [P, TT, D]) for i in range(2)]
        xT = sb("xT", [P, KD, S])
        rw = route_work(sb, "route", E)
        lg, ez, oh = rw[0], rw[2], rw[7]
        prob = sb("prob", [P, TOP, NTOK])
        names = ("weights", "xn_ready", "xT_turned", "xT_ready", "logits_done", "z_ready", "exp_ready", "kept", "own_v", "row_kept",
                 "counted", "places_ready", "scattered", "loaded0", "loaded1", "stored0", "stored1",
                 "x_turned", "x_ready", "up_done", "silu_ready", "hidden_ready", "h_turned", "hT_ready", "down_done", "out_ready",
                 "fetched0", "fetched1", "fetched2", "fetched3", "added", "experts_loaded")
        s = {n: sem(n) for n in names}
        lg_ps = PS[:, 1, 0:TT * E].rearrange("p (t e) -> p t e", t=TT)
        slot = sb("slot", [P, TOP, NTOK], U32)
        tile_expert = sb("tile_expert", [P, NT], I32)

        with ExitStack() as early:
            def sbe(name, shape, dt=F32):
                return early.enter_context(nc.sbuf_tensor(f"f3_{name}", shape, dt))
            rows = sbe("rows", [P, NTOK, D])
            oh_all = sbe("chosen_each", [P, TOP, NTOK, E])
            chosen = sbe("chosen", [P, NTOK, E])
            tmp = sbe("tmp", [P, TOP, TT, E])
            totals, upto = sbe("totals", [P, E, NTOK]), sbe("upto", [P, E, NTOK])
            first_zero, tile_starts = sbe("first_zero", [P, E, NTOK]), sbe("tile_starts", [P, NTOK])
            tiles_cmp = sbe("tiles_cmp", [P, E, NTOK])
            tiles, ends = sbe("tiles", [P, E]), sbe("ends", [P, E])
            place = sbe("place", [P, NTOK, E])
            slotf = sbe("slotf", [P, TOP, NTOK])
            past = sbe("past", [P, NT, E])
            expertf = sbe("expertf", [P, NT])
            ones = sbe("ones", [P, E])
            block = early.enter_context(nc.Block())

            @block.sync
            def _(sync):
                sync.dma_start(wr[:, :, :], io["L3_ffn_w_gate"].rearrange("(k p) e -> p k e", p=P)).then_inc(s["weights"], 16)
                for e in range(E):
                    for n in range(2):
                        sync.dma_start(w12[:, e, :, n, :], io[f"L3_ffn_w{n + 1}"][e].rearrange("(k p) h -> p k h", p=P)).then_inc(s["experts_loaded"], 16)
                    sync.dma_start(wc[:, e, :, :], io["L3_ffn_wc"][e].rearrange("(k p) d -> p k d", p=P)).then_inc(s["experts_loaded"], 16)

            @block.tensor
            def _(pe):
                def turn_x(b, par):
                    pe.wait_ge(s["xn_ready"], b + 1)
                    turn_tokens(pe, PS[:, 0, :], xn[par], ident).then_inc(s["xT_turned"], 1)

                def turn(b, par, last):
                    pe.wait_ge(s["xT_ready"], b + 1)
                    for t in range(TT):
                        for k in range(KD):
                            mm = pe.matmul(lg_ps[:, t, :], xT[:, k, t * P:(t + 1) * P], wr[:, k, :], start=(k == 0), stop=(k == KD - 1))
                    mm.then_inc(s["logits_done"], 1)
                    if not last:
                        turn_x(b + 1, 1 - par)

                pe.wait_ge(s["weights"], 16)
                turn_x(0, 0)
                in_pairs(pe, turn)
                pe.wait_ge(s["kept"], B)
                flat = chosen[:, :, :].rearrange("p t e -> p (t e)")
                pe.matmul(PS[:, 2, 0:NTOK * E], later_than[:, :], flat, start=True, stop=True)
                pe.matmul(PS[:, 3, 0:NTOK * E], all_ones[:, :], flat, start=True, stop=True).then_inc(s["counted"], 1)

            @block.scalar
            def _(act):
                def copy(b):
                    act.wait_ge(s["xT_turned"], b + 1)
                    act.activation(xT[:, :, :].rearrange("p k s -> p (k s)"), PS[:, 0, :], ACT.Copy).then_inc(s["xT_ready"], 1)

                def turn(b, par, last):
                    act.wait_ge(s["z_ready"], b + 1)
                    act.activation(ez[:, :, :], lg[:, :, :], ACT.Exp).then_inc(s["exp_ready"], 1)
                    if not last:
                        copy(b + 1)
                copy(0)
                in_pairs(act, turn)

            @block.gpsimd
            def _(pool):
                def turn(b, par, last):
                    wait_apart(pool, s["xn_ready"], b + 1, apart_pool)
                    pool.tensor_copy(rows[:, bass.ds(b * TT, TT), :], xn[par][:, :, :]).then_inc(s["row_kept"], 1)
                in_pairs(pool, turn)
                pool.wait_ge(s["row_kept"], B)
                pool.wait_ge(slots_zeroed, 16)
                pool.wait_ge(s["places_ready"], 1)
                for t in range(NTOK):
                    for k in range(TOP):
                        pool.indirect_dma_start(out=slots_in, out_offset=bass.IndirectOffsetOnAxis(ap=slot[:, k, t:t + 1], axis=0),
                                                in_=rows[:, t, :], in_offset=None).then_inc(s["scattered"], 16)
                pool.wait_ge(s["scattered"], 16 * NTOK * TOP)

            @block.vector
            def _(dve):
                TURN = ROUTE_STEPS + 3

                def turn(b, par, last):
                    st = Steps(dve, s["own_v"], LN_STEPS + b * (LN_STEPS + TURN), TURN + LN_STEPS * (not last))
                    if not last:
                        layer_norm(dve, st, X, b * TT + TT, work, xn[1 - par], s["xn_ready"], apart_v)
                    dve.wait_ge(s["logits_done"], b + 1)
                    route(dve, st, E, lg_ps, None, rw, iota, s["z_ready"], s["exp_ready"], b, apart_v)
                    st.step(dve.tensor_tensor(tmp[:, :, :, :], oh[:, :, :, :], bc(ez[:, None, :, :], [P, TOP, TT, E]), ALU.mult))
                    st.step(dve.tensor_reduce(prob[:, :, bass.ds(b * TT, TT)], tmp[:, :, :, :], AX.X, ALU.add))
                    dve.tensor_copy(oh_all[:, :, bass.ds(b * TT, TT), :], oh[:, :, :, :])
                    st.step(dve.tensor_tensor(chosen[:, bass.ds(b * TT, TT), :], oh[:, 0, :, :], oh[:, 1, :, :], ALU.add))
                    dve.wait_ge(s["row_kept"], b + 1)
                    dve.sem_inc(s["kept"], 1)
                    st.end()

                st = Steps(dve, s["own_v"], 0, LN_STEPS)
                layer_norm(dve, st, X, 0, work, xn[0], s["xn_ready"], apart_v)
                in_pairs(dve, turn)
                PLACE_STEPS = 16
                st = Steps(dve, s["own_v"], B * (LN_STEPS + TURN), PLACE_STEPS)
                dve.wait_ge(s["counted"], 1)
                dve.memset(first_zero[:, :, :], 1.0)
                dve.memset(ones[:, :], 1.0)
                st.step(dve.tensor_scalar(tile_starts[:, :], iota[:, 0:NTOK], float(P), None, ALU.mult))
                st.step(dve.memset(first_zero[:, :, 0:1], 0.0))
                st.step(dve.tensor_copy(totals[:, :, :], PS[:, 3, 0:NTOK * E].rearrange("p (t e) -> p e t", t=NTOK)))
                flat = lambda x: x[:, :, :].rearrange("p e t -> p (e t)")
                st.step(dve.tensor_tensor_scan(flat(upto), flat(first_zero), flat(totals), 0.0, ALU.mult, ALU.add))
                st.step(dve.tensor_tensor(tiles_cmp[:, :, :], bc(upto[:, :, NTOK - 1:NTOK], [P, E, NTOK]),
                                          bc(tile_starts[:, None, :], [P, E, NTOK]), ALU.is_gt))
                st.step(dve.tensor_reduce(tiles[:, :], tiles_cmp[:, :, :], AX.X, ALU.add))
                st.step(dve.tensor_tensor_scan(ends[:, :], ones[:, :], tiles[:, :], 0.0, ALU.mult, ALU.add))
                st.step(dve.tensor_tensor(upto[:, :, :], upto[:, :, :], totals[:, :, :], ALU.subtract))
                st.step(dve.tensor_tensor(tiles[:, :], ends[:, :], tiles[:, :], ALU.subtract))
                st.step(dve.scalar_tensor_tensor(upto[:, :, :], bc(tiles[:, :, None], [P, E, NTOK]), float(P), upto[:, :, :], ALU.mult, ALU.add))
                st.step(dve.tensor_tensor(place[:, :, :], upto[:, :, :].rearrange("p e t -> p t e"),
                                          PS[:, 2, 0:NTOK * E].rearrange("p (t e) -> p t e", t=NTOK), ALU.add))
                st.step(dve.tensor_tensor(oh_all[:, :, :, :], oh_all[:, :, :, :], bc(place[:, None, :, :], [P, TOP, NTOK, E]), ALU.mult))
                st.step(dve.tensor_reduce(slotf[:, :, :], oh_all[:, :, :, :], AX.X, ALU.add))
                dve.tensor_copy(slot[:, :, :], slotf[:, :, :]).then_inc(s["places_ready"], 1)
                st.step(dve.tensor_tensor(past[:, :, :], bc(iota[:, 0:NT, None], [P, NT, E]), bc(ends[:, None, :], [P, NT, E]), ALU.is_ge))
                st.step(dve.tensor_reduce(expertf[:, :], past[:, :, :], AX.X, ALU.add))
                st.step(dve.tensor_scalar(tile_expert[:, :], expertf[:, :], float(E - 1), None, ALU.min))
                st.end()

        xs = sb("slots_loaded", [P, 2, 2, D])
        sT = sb("slotsT", [P, 2, KD, P])
        gate, hid = sb("silu", [P, 2, H]), sb("hidden", [P, 2, H])
        hT = sb("hiddenT", [P, 2, KD, P])
        ys = sb("slots_out", [P, 2, 2, D])
        fetched = sb("fetched", [P, RING, TOP, D])
        block = ctx.enter_context(nc.Block())

        def tiles_of(view, g):
            n = min(2, NT - 2 * g) if isinstance(g, int) else 2
            return view.rearrange("(t p) d -> p t d", p=P)[:, bass.ds(2 * g, n), :], n

        @block.sync
        def _(sync):
            def load(g, par):
                src, n = tiles_of(slots_in, g)
                sync.dma_start(xs[:, par, 0:n, :], src).then_inc(s[f"loaded{par}"], 16)

            def store(g, par):
                dst, n = tiles_of(slots_out, g)
                sync.dma_start(dst, ys[:, par, 0:n, :]).then_inc(s[f"stored{par}"], 16)

            load(0, 0)
            load(1, 1)
            for g in range(NG + 2):
                if g + 2 < NG:
                    sync.wait_ge(s["x_turned"], 2 * g + 2)
                    load(g + 2, g % 2)
                if g >= 2:
                    sync.wait_ge(s["out_ready"], min(2 * g - 2, NT))
                    store(g - 2, g % 2)

        @block.tensor
        def _(pe):
            def expert(j):
                return nc.values_load(tile_expert[0:1, bass.ds(j, 1)], engines=[mybir.EngineType.PE], min_val=0, max_val=E - 1,
                                      skip_runtime_bounds_check_because="stage P takes the minimum with the last expert")

            def turn_slots(j, par, group, first):
                pe.wait_ge(s[f"loaded{group}"], first[0])
                if not first[1]:
                    pe.wait_ge(s["x_ready"], j - 1)
                for k in range(KD):
                    mm = pe.transpose(PS[:, 2 + par, k * P:(k + 1) * P], xs[:, group, par, k * P:(k + 1) * P], ident[:, :])
                mm.then_inc(s["x_turned"], 1)

            def up(j, par, early):
                e = expert(j)
                pe.wait_ge(s["x_ready"], j + 1)
                if not early:
                    pe.wait_ge(s["hidden_ready"], j - 1)
                for k in range(KD):
                    mm = pe.matmul(PS[:, par, :], sT[:, par, k, :], w12[:, bass.ds(e, 1), k, :, :].rearrange("p a n h -> p (a n h)"),
                                   start=(k == 0), stop=(k == KD - 1))
                mm.then_inc(s["up_done"], 1)

            def turn_hidden(j, par, early):
                pe.wait_ge(s["hidden_ready"], j + 1)
                if not early:
                    pe.wait_ge(s["hT_ready"], j - 1)
                for k in range(KD):
                    mm = pe.transpose(PS[:, 4 + par, k * P:(k + 1) * P], hid[:, par, k * P:(k + 1) * P], ident[:, :])
                mm.then_inc(s["h_turned"], 1)

            def down(j, par, early):
                e = expert(j)
                pe.wait_ge(s["hT_ready"], j + 1)
                if not early:
                    pe.wait_ge(s["out_ready"], j - 1)
                for k in range(KD):
                    mm = pe.matmul(PS[:, 6 + par, 0:D], hT[:, par, k, :], wc[:, bass.ds(e, 1), k, :].rearrange("p a d -> p (a d)"),
                                   start=(k == 0), stop=(k == KD - 1))
                mm.then_inc(s["down_done"], 1)

            def step(j, i, quad, head=False, tail=False):
                par = i % 2
                fixed = isinstance(j, int)
                if not (fixed and j >= NT):
                    up(j, par, fixed and j < 2)
                if not (fixed and not 1 <= j < NT + 1):
                    turn_hidden(j - 1, 1 - par, fixed and j - 1 < 2)
                if not (fixed and j + 1 >= NT):
                    ni = i + 1
                    turn_slots(j + 1, 1 - par, (ni // 2) % 2, (16 * (quad + ni // 4 + 1), fixed and j + 1 < 2))
                if not (fixed and j < 2):
                    down(j - 2, par, fixed and j - 2 < 2)

            pe.wait_ge(s["experts_loaded"], 16 * 3 * E)
            turn_slots(0, 0, 0, (16, True))
            for i in range(4):
                step(i, i, 0)
            with pe.Fori(1, NT // 4) as quad:
                for i in range(4):
                    step(4 * quad + i, i, quad)
            for j in range(NT - NT % 4, NT + 2):
                step(j, j % 4, j // 4)

        @block.scalar
        def _(act):
            def silu(j, par, early):
                act.wait_ge(s["up_done"], j + 1)
                if not early:
                    act.wait_ge(s["hidden_ready"], j - 1)
                act.activation(gate[:, par, :], PS[:, par, 0:H], ACT.Silu).then_inc(s["silu_ready"], 1)

            def hidden(j, par, early):
                act.wait_ge(s["h_turned"], j + 1)
                if not early:
                    act.wait_ge(s["down_done"], j - 1)
                act.activation(hT[:, par, :, :].rearrange("p k n -> p (k n)"), PS[:, 4 + par, 0:H], ACT.Copy).then_inc(s["hT_ready"], 1)

            def output(j, par, group, stored):
                act.wait_ge(s["down_done"], j + 1)
                if stored is not None:
                    act.wait_ge(s[f"stored{group}"], stored)
                act.activation(ys[:, group, par, :], PS[:, 6 + par, 0:D], ACT.Copy).then_inc(s["out_ready"], 1)

            def step(j, i, quad):
                par = i % 2
                fixed = isinstance(j, int)
                if not (fixed and j >= NT):
                    silu(j, par, fixed and j < 2)
                if not (fixed and not 1 <= j < NT + 1):
                    hidden(j - 1, 1 - par, fixed and j - 1 < 2)
                if not (fixed and j < 2):
                    q, pi = (quad, i - 2) if i >= 2 else (quad - 1, i + 2)
                    output(j - 2, par, pi // 2, None if fixed and j - 2 < 4 else 16 * q)
            for i in range(8):
                step(i, i % 4, i // 4)
            with act.Fori(2, NT // 4) as quad:
                for i in range(4):
                    step(4 * quad + i, i, quad)
            for j in range(NT - NT % 4, NT + 2):
                step(j, j % 4, j // 4)

        @block.gpsimd
        def _(pool):
            pool.wait_ge(s["stored0"], 16 * ((NG + 1) // 2))
            pool.wait_ge(s["stored1"], 16 * (NG // 2))
            for t in range(NTOK):
                if t >= RING:
                    pool.wait_ge(s["added"], t - RING + 1)
                for k in range(TOP):
                    pool.indirect_dma_start(out=fetched[:, t % RING, k, :], out_offset=None, in_=slots_out,
                                            in_offset=bass.IndirectOffsetOnAxis(ap=slot[:, k, t:t + 1], axis=0)).then_inc(s[f"fetched{t % RING}"], 16)

        @block.vector
        def _(dve):
            def copy_slots(j, par, early):
                dve.wait_ge(s["x_turned"], j + 1)
                if not early:
                    dve.wait_ge(s["up_done"], j - 1)
                dve.tensor_copy(sT[:, par, :, :].rearrange("p k n -> p (k n)"), PS[:, 2 + par, 0:D]).then_inc(s["x_ready"], 1)

            def step(j, par):
                fixed = isinstance(j, int)
                dve.wait_ge(s["silu_ready"], j + 1)
                if not (fixed and j < 2):
                    dve.wait_ge(s["h_turned"], j - 1)
                dve.tensor_tensor(hid[:, par, :], gate[:, par, :], PS[:, par, H:2 * H], ALU.mult).then_inc(s["hidden_ready"], 1)
                if not (fixed and j + 1 >= NT):
                    copy_slots(j + 1, 1 - par, fixed and j + 1 < 2)
            copy_slots(0, 0, True)
            step(0, 0)
            step(1, 1)
            with dve.Fori(1, NT // 2) as pair:
                for par in range(2):
                    step(2 * pair + par, par)
            for j in range(NT - NT % 2, NT):
                step(j, j % 2)
            for t in range(NTOK):
                for k in range(TOP):
                    if k == 0:
                        dve.wait_ge(s[f"fetched{t % RING}"], 16 * TOP * (t // RING + 1))
                    i = dve.scalar_tensor_tensor(X[:, t, :], fetched[:, t % RING, k, :], prob[:, k, t:t + 1], X[:, t, :], ALU.mult, ALU.add)
                    if k == 0:
                        i.then_inc(s["kept"], 1)
                        dve.wait_ge(s["kept"], B + t + 1)
                i.then_inc(s["added"], 1)

def build_phases(nc, io, out, phases):
    with ExitStack() as ctx:
        PS = ctx.enter_context(nc.psum_tensor("banks", [P, 8, 512], F32))
        bank = [PS[:, i, :] for i in range(8)]
        sp = Space(nc, ctx, "all")
        X = sp.sb("x", [P, B * TT, D])
        C = sp.sb("ctx", [P, B * TT, D])
        CT = sp.sb("ctxT", [P, KD, B * S])
        ident = sp.sb("ident", [P, P])
        identb = sp.sb("identb", [P, P], BF16)
        iota = sp.sb("iota", [P, 512])
        all_ones, later_than = sp.sb("all_ones", [P, P]), sp.sb("later_than", [P, P])
        loaded, made, stored = sp.sem("loaded"), sp.sem("constants_made"), sp.sem("stored")
        apart = sp.sem("vector_apart")
        apart_pool, apart_sync, apart_pe = sp.sem("pool_apart"), sp.sem("sync_apart"), sp.sem("tensor_apart")
        zero_row, slots_zeroed = sp.sb("zero_row", [P, D]), sp.sem("slots_zeroed")
        io = dict(io)
        for name in ("slots_in", "slots_out"):
            io[name] = nc.dram_tensor(name, (SLOT_TILES * P, D), F32, kind="Internal").ap()
        turned, turned_copied = sp.sem("ctx_turned"), sp.sem("ctx_copied")
        with nc.Block() as block:
            @block.sync
            def _(sync):
                sync.dma_start(X[:, :, :], io["x"].rearrange("b (t p) d -> p (b t) d", p=P)).then_inc(loaded, 16)
                sync.dma_start(C[:, :, :], io["ctx_1024"].rearrange("b (t p) d -> p (b t) d", p=P)).then_inc(loaded, 16)
                sync.wait_ge(made, MADE + 1)
                sync.dma_start(io["slots_in"].rearrange("(t p) d -> p t d", p=P),
                               zero_row[:, None, :].to_broadcast([P, SLOT_TILES, D])).then_inc(slots_zeroed, 16)
                sync.wait_ge(loaded, 32)

            @block.gpsimd
            def _(pool):
                pool.memset(ident[:, :], 0.0).then_inc(made, 1)
                pool.iota(iota[:, :], pattern=[[1, 512]], base=0, channel_multiplier=0,
                          allow_small_or_imprecise_dtypes=True)
                pool.wait_ge(made, 1)
                pool.affine_select(out=ident[:, :], in_=ident[:, :], compare_op=ALU.not_equal, fill=1.0,
                                   base=0, pattern=[[-1, P]], channel_multiplier=1).then_inc(made, 1)
                pool.wait_ge(made, 2)
                pool.tensor_copy(identb[:, :], ident[:, :]).then_inc(made, 1)
                pool.wait_ge(made, 3)
                pool.memset(all_ones[:, :], 1.0).then_inc(made, 1)
                pool.wait_ge(made, 4)
                pool.affine_select(out=later_than[:, :], in_=all_ones[:, :], compare_op=ALU.is_gt, fill=0.0,
                                   base=0, pattern=[[1, P]], channel_multiplier=-1).then_inc(made, 1)
                pool.wait_ge(made, MADE)
                pool.memset(zero_row[:, :], 0.0).then_inc(made, 1)

            @block.tensor
            def _(pe):
                pe.wait_ge(loaded, 32)
                pe.wait_ge(made, MADE)
                for b in range(B):
                    if b >= 2:
                        pe.wait_ge(turned_copied, b - 1)
                    turn_tokens(pe, bank[b % 2], C[:, b * TT:(b + 1) * TT, :], ident).then_inc(turned, 1)

            @block.vector
            def _(dve):
                for b in range(B):
                    dve.wait_ge(turned, b + 1)
                    dve.tensor_copy(CT[:, :, b * S:(b + 1) * S], bank[b % 2].rearrange("p (k s) -> p k s", k=KD)).then_inc(turned_copied, 1)

        T = {2: lambda: phase_ffn0(nc, io, X, bank, ident, iota, apart),
             1: lambda: phase_mlstm(nc, io, X, C, CT, PS, ident, identb, (apart, apart_pool, apart_sync, apart_pe)),
             3: lambda: phase_attention(nc, io, X, C, CT, PS, ident, iota, (apart, apart_pool, apart_sync, apart_pe), 1),
             6: lambda: phase_ffn2(nc, io, X, PS, ident, iota, (apart, apart_pool, apart_sync, apart_pe), later_than, all_ones),
             4: lambda: phase_ffn1(nc, io, X, PS, ident, iota, (apart, apart_pool, apart_sync, apart_pe)),
             8: lambda: phase_ffn3(nc, io, X, PS, ident, iota, (apart, apart_pool, apart_sync, apart_pe), later_than, all_ones, slots_zeroed),
             5: lambda: phase_attention(nc, io, X, C, CT, PS, ident, iota, (apart, apart_pool, apart_sync, apart_pe), 2),
             7: lambda: phase_attention(nc, io, X, C, CT, PS, ident, iota, (apart, apart_pool, apart_sync, apart_pe), 3)}
        for p in phases:
            T[p]()
        with nc.Block() as block:
            @block.sync
            def _(sync):
                sync.dma_start(out.rearrange("b (t p) d -> p (b t) d", p=P), X[:, :, :]).then_inc(stored, 16)
                sync.wait_ge(stored, 16)


def lay_out(inputs):
    import numpy as np
    put = {k: np.ascontiguousarray(v) for k, v in inputs.items()}
    for name in ("L1_xattn_Wq", "L1_xattn_Wkv", "L1_xattn_Wc", "L2_xattn_Wq", "L2_xattn_Wk", "L2_xattn_Wc"):
        put[name + "T"] = np.ascontiguousarray(put.pop(name).T)
    for name in ("L0_xattn_igate_w", "L0_xattn_fgate_w"):
        put[name + "T"] = np.ascontiguousarray(put.pop(name).T)
    put["itokT"] = np.ascontiguousarray(put.pop("itok_SxS2_0_2016").T).view(np.uint32)
    put["L1_ffn_WrT"] = np.ascontiguousarray(put.pop("L1_ffn_Wr").T)
    n_rotate, head = 64, 128
    half = n_rotate // 2
    inv_freq = np.float32(1.0) / np.power(np.float32(10000.0), np.arange(half, dtype=np.float32) * np.float32(2.0) / np.float32(n_rotate))
    angle = np.arange(S, dtype=np.float32)[:, None] * inv_freq.astype(np.float32)
    cos, sin = np.cos(angle), np.sin(angle)
    put["rope_table"] = np.concatenate([cos, cos, np.ones((S, head - n_rotate)), -sin, sin], axis=1).astype(np.float32)
    return put


def eight_blocks(nc, io, out):
    build_phases(nc, io, out, range(1, 9))


def kernel(**inputs):
    import numpy as np
    import concourse.bacc as bacc
    from concourse.bass_utils import run_bass_kernel_spmd

    nc = bacc.Bacc("TRN2", target_bir_lowering=False, num_devices=1)
    put = lay_out({name: np.asarray(a) for name, a in inputs.items()})
    io = {name: nc.dram_tensor(f"in_{name}", a.shape, mybir.dt.from_np(a.dtype), kind="ExternalInput").ap()
          for name, a in put.items()}
    out = nc.dram_tensor("out_0_dram", (B, S, D), F32, kind="ExternalOutput").ap()
    eight_blocks(nc, io, out)
    result = run_bass_kernel_spmd(nc, [{f"in_{name}": a for name, a in put.items()}], core_ids=[0])
    return result.results[0]["out_0_dram"]
```
